# Optimizing a Trainium2 kernel written in Bass

```python
import numpy as np
import jax
import jax.numpy as jnp

def _softmax(x, axis=-1):
    return jax.nn.softmax(x, axis=axis)

def _gelu(x):
    return jax.nn.gelu(x, approximate=True)

def _silu(x):
    return jax.nn.silu(x)

def _sigmoid(x):
    return jax.nn.sigmoid(x)

def _layernorm(x, axis=-1, eps=1e-05):
    m = jnp.mean(x, axis=axis, keepdims=True)
    v = jnp.var(x, axis=axis, keepdims=True)
    return (x - m) / jnp.sqrt(v + eps)

def _scatter_add(tgt, idx, src, axis=0):
    return tgt.at[idx].add(src)

def _segment_sum(src, seg, n):
    return jax.ops.segment_sum(src, seg, n)
kernel_name = 'mk_seq_postln_d2_jaxref_r8_7b22fc'

def setup_inputs(seed: int=0):
    np.random.seed(seed)
    _w = jnp.asarray

    def _L0_attn_setup():
        import jax, jax.numpy as jnp
        import numpy as np
        from jax import lax
        B, T, H = (4, 256, 128)
        HU = 4 * H
        LAYERS, INDEX = (12, 0)
        K_CLAMP, K_EPS = (60.0, 1e-08)
        LN_EPS = 1e-05

        def _ln(x, g, b):
            m = jnp.mean(x, -1, keepdims=True)
            v = jnp.mean((x - m) ** 2, -1, keepdims=True)
            return (x - m) / jnp.sqrt(v + LN_EPS) * g + b

        def _shift(x):
            return jnp.pad(x[:, :-1], ((0, 0), (1, 0), (0, 0)))

        def _wkv(k, kv, decay, first):

            def step(carry, inp):
                sk, skv = carry
                kt, kvt = inp
                out = (first * kt + sk, first * kvt + skv)
                return ((kt + decay * sk, kvt + decay * skv), out)
            b = k.shape[0]
            init = (jnp.zeros((b, k.shape[2]), k.dtype), jnp.zeros((b, k.shape[2]), k.dtype))
            _, (wk, wkv) = lax.scan(step, init, (jnp.swapaxes(k, 0, 1), jnp.swapaxes(kv, 0, 1)))
            return (jnp.swapaxes(wk, 0, 1), jnp.swapaxes(wkv, 0, 1))
        key = jax.random.key(seed)
        ks = jax.random.split(key, 9)
        s = 0.02
        tr01 = INDEX / (LAYERS - 1)
        tr1pz = 1.0 - INDEX / LAYERS
        i_h = np.arange(H, dtype=np.float64) / H
        i_hu = np.arange(HU, dtype=np.float64)
        decay_speed = -5.0 + 8.0 * (i_hu / (HU - 1)) ** (0.7 + 1.3 * tr01)
        zigzag = ((np.arange(HU) + 1) % 3 - 1) * 0.5
        time_first = np.log(0.3) + zigzag
        f32 = lambda a: jnp.asarray(a, jnp.float32)
        return {'x': jax.random.normal(ks[0], (B, T, H), jnp.float32), 'ln0_g': jnp.ones((H,), jnp.float32), 'ln0_b': jnp.zeros((H,), jnp.float32), 'pre_g': jnp.ones((H,), jnp.float32), 'pre_b': jnp.zeros((H,), jnp.float32), 'post_g': jnp.ones((H,), jnp.float32), 'post_b': jnp.zeros((H,), jnp.float32), 'tm_decay': f32(decay_speed), 'tm_first': f32(time_first), 'tm_mix_k': f32(i_h ** tr1pz), 'tm_mix_v': f32(i_h ** tr1pz + 0.3 * tr01), 'tm_mix_r': f32(i_h ** (0.5 * tr1pz)), 'tm_Wk': jax.random.normal(ks[1], (H, HU), jnp.float32) * s, 'tm_Wv': jax.random.normal(ks[2], (H, HU), jnp.float32) * s, 'tm_Wr': jax.random.normal(ks[3], (H, HU), jnp.float32) * s, 'tm_Wo': jax.random.normal(ks[4], (HU, H), jnp.float32) * s, 'cm_mix_k': f32(i_h ** tr1pz), 'cm_mix_r': f32(i_h ** tr1pz), 'cm_Wk': jax.random.normal(ks[5], (H, HU), jnp.float32) * s, 'cm_Wv': jax.random.normal(ks[6], (HU, H), jnp.float32) * s, 'cm_Wr': jax.random.normal(ks[7], (H, H), jnp.float32) * s}
    _L0_attn_in = _L0_attn_setup()

    def _L0_ffn_setup():
        import jax, jax.numpy as jnp
        import numpy as np
        D_MODEL = 128
        DEPTH = 8
        M = 2 ** DEPTH
        N_INTERNAL = M - 1
        B, T = (8, 512)

        def _leaf_probs(gate):
            BT = gate.shape[0]
            lp = jnp.ones((BT, M), dtype=gate.dtype)
            for level in range(DEPTH):
                n = 2 ** level
                half = M // (2 * n)
                g = gate[:, n - 1:2 * n - 1]
                f = jnp.stack([1.0 - g, g], axis=-1)
                f = jnp.broadcast_to(f[..., None], (BT, n, 2, half))
                lp = lp * f.reshape(BT, M)
            return lp
        key = jax.random.key(seed)
        ks = jax.random.split(key, 7)
        x = jax.random.normal(ks[0], (B, T, D_MODEL), dtype=jnp.float32)
        Wq = jax.random.normal(ks[1], (D_MODEL, D_MODEL), dtype=jnp.float32) * 0.02
        routers = jax.random.normal(ks[2], (N_INTERNAL, D_MODEL), dtype=jnp.float32) * 0.02
        leaf_keys = jax.random.normal(ks[3], (M, D_MODEL), dtype=jnp.float32) * 0.02
        leaf_values = jax.random.normal(ks[4], (M, D_MODEL), dtype=jnp.float32) * 0.02
        Wout_w = jax.random.normal(ks[5], (D_MODEL, D_MODEL), dtype=jnp.float32) * 0.02
        Wout_b = jax.random.normal(ks[6], (D_MODEL,), dtype=jnp.float32) * 0.02
        return {'x': x, 'Wq': Wq, 'routers': routers, 'leaf_keys': leaf_keys, 'leaf_values': leaf_values, 'Wout_w': Wout_w, 'Wout_b': Wout_b}
    _L0_ffn_in = _L0_ffn_setup()

    def _L1_attn_setup():
        import jax, jax.numpy as jnp
        import numpy as np
        ROPE_BASE = 1000000.0
        EPS = 1e-06
        N_HEADS = 16

        def apply_rope(x, base=ROPE_BASE):
            b, seq, n_heads, dim = x.shape
            half = dim // 2
            i = jnp.arange(half)
            theta = 1.0 / base ** (2 * i / dim)
            pos = jnp.arange(seq)
            angles = pos[:, None] * theta[None, :]
            cos = jnp.cos(angles)[None, :, None, :]
            sin = jnp.sin(angles)[None, :, None, :]
            x1, x2 = jnp.split(x, 2, axis=-1)
            return jnp.concatenate([x1 * cos - x2 * sin, x1 * sin + x2 * cos], axis=-1)
        key = jax.random.key(seed)
        ks = jax.random.split(key, 6)
        b, seq, dim = (2, 256, 128)
        scale = 1.0 / np.sqrt(dim)
        return {'x': jax.random.normal(ks[0], (b, seq, dim), dtype=jnp.float32), 'norm_scale': jnp.ones((dim,), dtype=jnp.float32), 'Wq': jax.random.normal(ks[1], (dim, dim), dtype=jnp.float32) * scale, 'Wk': jax.random.normal(ks[2], (dim, dim), dtype=jnp.float32) * scale, 'Wv': jax.random.normal(ks[3], (dim, dim), dtype=jnp.float32) * scale, 'Wo': jax.random.normal(ks[4], (dim, dim), dtype=jnp.float32) * scale}
    _L1_attn_in = _L1_attn_setup()

    def _L1_ffn_setup():
        import jax, jax.numpy as jnp
        import numpy as np
        TOP_K = 2
        key = jax.random.key(seed)
        ks = jax.random.split(key, 8)
        B, S, D = (2, 256, 128)
        N_r, N_s = (16, 2)
        u = jax.random.normal(ks[0], (B, S, D), dtype=jnp.float32)
        centroids = jax.random.normal(ks[1], (N_r, D), dtype=jnp.float32)
        expert_biases = jnp.zeros((N_r,), dtype=jnp.float32)
        Wr = jax.random.normal(ks[2], (N_r, D, D), dtype=jnp.float32) * (1.0 / np.sqrt(D))
        br = jax.random.normal(ks[3], (N_r, D), dtype=jnp.float32) * 0.01
        Ws = jax.random.normal(ks[4], (N_s, D, D), dtype=jnp.float32) * (1.0 / np.sqrt(D))
        bs = jax.random.normal(ks[5], (N_s, D), dtype=jnp.float32) * 0.01
        return {'u': u, 'centroids': centroids, 'expert_biases': expert_biases, 'Wr': Wr, 'br': br, 'Ws': Ws, 'bs': bs}
    _L1_ffn_in = _L1_ffn_setup()
    _d = {'L0_attn_x': _L0_attn_in['x'], 'L0_attn_ln0_g': _L0_attn_in['ln0_g'], 'L0_attn_ln0_b': _L0_attn_in['ln0_b'], 'L0_attn_pre_g': _L0_attn_in['pre_g'], 'L0_attn_pre_b': _L0_attn_in['pre_b'], 'L0_attn_post_g': _L0_attn_in['post_g'], 'L0_attn_post_b': _L0_attn_in['post_b'], 'L0_attn_tm_decay': _L0_attn_in['tm_decay'], 'L0_attn_tm_first': _L0_attn_in['tm_first'], 'L0_attn_tm_mix_k': _L0_attn_in['tm_mix_k'], 'L0_attn_tm_mix_v': _L0_attn_in['tm_mix_v'], 'L0_attn_tm_mix_r': _L0_attn_in['tm_mix_r'], 'L0_attn_tm_Wk': _L0_attn_in['tm_Wk'], 'L0_attn_tm_Wv': _L0_attn_in['tm_Wv'], 'L0_attn_tm_Wr': _L0_attn_in['tm_Wr'], 'L0_attn_tm_Wo': _L0_attn_in['tm_Wo'], 'L0_attn_cm_mix_k': _L0_attn_in['cm_mix_k'], 'L0_attn_cm_mix_r': _L0_attn_in['cm_mix_r'], 'L0_attn_cm_Wk': _L0_attn_in['cm_Wk'], 'L0_attn_cm_Wv': _L0_attn_in['cm_Wv'], 'L0_attn_cm_Wr': _L0_attn_in['cm_Wr'], 'L0_ffn_Wq': _L0_ffn_in['Wq'], 'L0_ffn_routers': _L0_ffn_in['routers'], 'L0_ffn_leaf_keys': _L0_ffn_in['leaf_keys'], 'L0_ffn_leaf_values': _L0_ffn_in['leaf_values'], 'L0_ffn_Wout_w': _L0_ffn_in['Wout_w'], 'L0_ffn_Wout_b': _L0_ffn_in['Wout_b'], 'L1_attn_norm_scale': _L1_attn_in['norm_scale'], 'L1_attn_Wq': _L1_attn_in['Wq'], 'L1_attn_Wk': _L1_attn_in['Wk'], 'L1_attn_Wv': _L1_attn_in['Wv'], 'L1_attn_Wo': _L1_attn_in['Wo'], 'L1_ffn_centroids': _L1_ffn_in['centroids'], 'L1_ffn_expert_biases': _L1_ffn_in['expert_biases'], 'L1_ffn_Wr': _L1_ffn_in['Wr'], 'L1_ffn_br': _L1_ffn_in['br'], 'L1_ffn_Ws': _L1_ffn_in['Ws'], 'L1_ffn_bs': _L1_ffn_in['bs']}
    _x0 = _d['L0_attn_x']
    _d['L0_attn_x'] = jax.random.normal(jax.random.fold_in(jax.random.key(seed), 1), (16, 512, 128), dtype=_x0.dtype)
    del _x0
    return _d

def reference(L0_attn_x, L0_attn_ln0_g, L0_attn_ln0_b, L0_attn_pre_g, L0_attn_pre_b, L0_attn_post_g, L0_attn_post_b, L0_attn_tm_decay, L0_attn_tm_first, L0_attn_tm_mix_k, L0_attn_tm_mix_v, L0_attn_tm_mix_r, L0_attn_tm_Wk, L0_attn_tm_Wv, L0_attn_tm_Wr, L0_attn_tm_Wo, L0_attn_cm_mix_k, L0_attn_cm_mix_r, L0_attn_cm_Wk, L0_attn_cm_Wv, L0_attn_cm_Wr, L0_ffn_Wq, L0_ffn_routers, L0_ffn_leaf_keys, L0_ffn_leaf_values, L0_ffn_Wout_w, L0_ffn_Wout_b, L1_attn_norm_scale, L1_attn_Wq, L1_attn_Wk, L1_attn_Wv, L1_attn_Wo, L1_ffn_centroids, L1_ffn_expert_biases, L1_ffn_Wr, L1_ffn_br, L1_ffn_Ws, L1_ffn_bs):

    def _L0_attn_ref(x, ln0_g, ln0_b, pre_g, pre_b, post_g, post_b, tm_decay, tm_first, tm_mix_k, tm_mix_v, tm_mix_r, tm_Wk, tm_Wv, tm_Wr, tm_Wo, cm_mix_k, cm_mix_r, cm_Wk, cm_Wv, cm_Wr):
        import jax, jax.numpy as jnp
        import numpy as np
        from jax import lax
        B, T, H = (4, 256, 128)
        HU = 4 * H
        LAYERS, INDEX = (12, 0)
        K_CLAMP, K_EPS = (60.0, 1e-08)
        LN_EPS = 1e-05

        def _ln(x, g, b):
            m = jnp.mean(x, -1, keepdims=True)
            v = jnp.mean((x - m) ** 2, -1, keepdims=True)
            return (x - m) / jnp.sqrt(v + LN_EPS) * g + b

        def _shift(x):
            return jnp.pad(x[:, :-1], ((0, 0), (1, 0), (0, 0)))

        def _wkv(k, kv, decay, first):

            def step(carry, inp):
                sk, skv = carry
                kt, kvt = inp
                out = (first * kt + sk, first * kvt + skv)
                return ((kt + decay * sk, kvt + decay * skv), out)
            b = k.shape[0]
            init = (jnp.zeros((b, k.shape[2]), k.dtype), jnp.zeros((b, k.shape[2]), k.dtype))
            _, (wk, wkv) = lax.scan(step, init, (jnp.swapaxes(k, 0, 1), jnp.swapaxes(kv, 0, 1)))
            return (jnp.swapaxes(wk, 0, 1), jnp.swapaxes(wkv, 0, 1))
        if INDEX == 0:
            x = _ln(x, ln0_g, ln0_b)
        xn = _ln(x, pre_g, pre_b)
        xx = _shift(xn)
        xk = xn * tm_mix_k + xx * (1.0 - tm_mix_k)
        xv = xn * tm_mix_v + xx * (1.0 - tm_mix_v)
        xr = xn * tm_mix_r + xx * (1.0 - tm_mix_r)
        k = jnp.exp(jnp.minimum(xk @ tm_Wk, K_CLAMP))
        v = xv @ tm_Wv
        r = xr @ tm_Wr
        kv = k * v
        decay = jnp.exp(-jnp.exp(tm_decay))
        first = jnp.exp(tm_first)
        wk, wkv = _wkv(k, kv, decay, first)
        rwkv = jax.nn.sigmoid(r) * (wkv / (wk + K_EPS))
        x = x + rwkv @ tm_Wo
        xn = _ln(x, post_g, post_b)
        xx = _shift(xn)
        xk = xn * cm_mix_k + xx * (1.0 - cm_mix_k)
        xr = xn * cm_mix_r + xx * (1.0 - cm_mix_r)
        kv = jax.nn.silu(xk @ cm_Wk) @ cm_Wv
        x = x + (jax.nn.sigmoid(xr @ cm_Wr) + kv)
        return x

    def _L0_ffn_ref(x, Wq, routers, leaf_keys, leaf_values, Wout_w, Wout_b):
        import jax, jax.numpy as jnp
        import numpy as np
        D_MODEL = 128
        DEPTH = 8
        M = 2 ** DEPTH
        N_INTERNAL = M - 1
        B, T = (8, 512)

        def _leaf_probs(gate):
            BT = gate.shape[0]
            lp = jnp.ones((BT, M), dtype=gate.dtype)
            for level in range(DEPTH):
                n = 2 ** level
                half = M // (2 * n)
                g = gate[:, n - 1:2 * n - 1]
                f = jnp.stack([1.0 - g, g], axis=-1)
                f = jnp.broadcast_to(f[..., None], (BT, n, 2, half))
                lp = lp * f.reshape(BT, M)
            return lp
        Bv, Tv, d = x.shape
        q = jnp.einsum('btd,ed->bte', x, Wq)
        q_flat = q.reshape(Bv * Tv, d)
        gate = jax.nn.sigmoid(q_flat @ routers.T)
        leaf_prob = _leaf_probs(gate)
        ret = (leaf_prob @ leaf_values).reshape(Bv, Tv, d)
        return jnp.einsum('btd,ed->bte', ret, Wout_w) + Wout_b

    def _L1_attn_ref(x, norm_scale, Wq, Wk, Wv, Wo):
        import jax, jax.numpy as jnp
        import numpy as np
        ROPE_BASE = 1000000.0
        EPS = 1e-06
        N_HEADS = 16

        def apply_rope(x, base=ROPE_BASE):
            b, seq, n_heads, dim = x.shape
            half = dim // 2
            i = jnp.arange(half)
            theta = 1.0 / base ** (2 * i / dim)
            pos = jnp.arange(seq)
            angles = pos[:, None] * theta[None, :]
            cos = jnp.cos(angles)[None, :, None, :]
            sin = jnp.sin(angles)[None, :, None, :]
            x1, x2 = jnp.split(x, 2, axis=-1)
            return jnp.concatenate([x1 * cos - x2 * sin, x1 * sin + x2 * cos], axis=-1)
        b, seq, d = x.shape
        n_heads = N_HEADS
        dh = d // n_heads
        var = jnp.mean(jnp.square(x), axis=-1, keepdims=True)
        x_norm = x * jax.lax.rsqrt(var + EPS) * norm_scale
        q = (x_norm @ Wq).reshape(b, seq, n_heads, dh)
        k = (x_norm @ Wk).reshape(b, seq, n_heads, dh)
        v = (x_norm @ Wv).reshape(b, seq, n_heads, dh)
        q = apply_rope(q)
        k = apply_rope(k)
        scores = jnp.einsum('bthd,bshd->bhts', q, k) / jnp.sqrt(jnp.float32(dh))
        causal = jnp.triu(jnp.full((seq, seq), -jnp.inf, dtype=jnp.float32), k=1)
        scores = scores + causal[None, None, :, :]
        weights = jax.nn.softmax(scores, axis=-1)
        out = jnp.einsum('bhts,bshd->bthd', weights, v).reshape(b, seq, d)
        return out @ Wo

    def _L1_ffn_ref(u, centroids, expert_biases, Wr, br, Ws, bs):
        import jax, jax.numpy as jnp
        import numpy as np
        TOP_K = 2
        N_r = centroids.shape[0]
        N_s = Ws.shape[0]
        raw_scores = jnp.einsum('bsd,ed->bse', u, centroids)
        s = jax.nn.softmax(raw_scores + expert_biases, axis=-1)
        topk_vals, topk_idx = jax.lax.top_k(s, TOP_K)
        g_topk = jnp.sum(jax.nn.one_hot(topk_idx, N_r, dtype=s.dtype) * topk_vals[..., None], axis=-2)
        xe = jnp.einsum('bsd,eod->bseo', u, Wr) + br
        routed = jnp.einsum('bse,bseo->bso', g_topk, xe)
        shared = (jnp.einsum('bsd,eod->bso', u, Ws) + jnp.sum(bs, axis=0)) / N_s
        return u + routed + shared
    x = L0_attn_x
    x = _layernorm(x + _L0_attn_ref(x, L0_attn_ln0_g, L0_attn_ln0_b, L0_attn_pre_g, L0_attn_pre_b, L0_attn_post_g, L0_attn_post_b, L0_attn_tm_decay, L0_attn_tm_first, L0_attn_tm_mix_k, L0_attn_tm_mix_v, L0_attn_tm_mix_r, L0_attn_tm_Wk, L0_attn_tm_Wv, L0_attn_tm_Wr, L0_attn_tm_Wo, L0_attn_cm_mix_k, L0_attn_cm_mix_r, L0_attn_cm_Wk, L0_attn_cm_Wv, L0_attn_cm_Wr), axis=-1)
    x = _layernorm(x + _L0_ffn_ref(x, L0_ffn_Wq, L0_ffn_routers, L0_ffn_leaf_keys, L0_ffn_leaf_values, L0_ffn_Wout_w, L0_ffn_Wout_b), axis=-1)
    x = _layernorm(x + _L1_attn_ref(x, L1_attn_norm_scale, L1_attn_Wq, L1_attn_Wk, L1_attn_Wv, L1_attn_Wo), axis=-1)
    x = _layernorm(x + _L1_ffn_ref(x, L1_ffn_centroids, L1_ffn_expert_biases, L1_ffn_Wr, L1_ffn_br, L1_ffn_Ws, L1_ffn_bs), axis=-1)
    return x

_drawn_inputs = setup_inputs


def setup_inputs(seed=0):
    import zlib

    import numpy as np

    out = dict(_drawn_inputs(seed))
    spreads = {'L0_attn_ln0_g': (1.0, 0.2),
     'L0_attn_ln0_b': (0.0, 0.1),
     'L0_attn_pre_g': (1.0, 0.6),
     'L0_attn_pre_b': (0.0, 0.8),
     'L0_attn_post_g': (1.0, 0.6),
     'L0_attn_post_b': (0.0, 0.712),
     'L1_attn_norm_scale': (1.0, 0.2),
     'L1_ffn_expert_biases': (0.0, 0.552)}
    factors = {'L0_attn_tm_decay': 3.371,
     'L0_attn_tm_first': 200.0,
     'L0_attn_tm_mix_k': 8.0,
     'L0_attn_tm_mix_v': 5.263,
     'L0_attn_tm_mix_r': 8.0,
     'L0_attn_tm_Wk': 8.0,
     'L0_attn_tm_Wr': 8.0,
     'L0_attn_cm_mix_k': 2.692,
     'L0_ffn_Wq': 8.0,
     'L0_ffn_routers': 8.0,
     'L0_ffn_leaf_values': 8.0,
     'L0_ffn_Wout_w': 8.0,
     'L1_ffn_br': 8.0,
     'L1_ffn_bs': 8.0}
    for name, (base, spread) in spreads.items():
        noise = np.random.default_rng([zlib.crc32(name.encode()), seed]).standard_normal(out[name].shape)
        drawn = base * np.exp(spread * noise) if base else spread * noise
        out[name] = jnp.asarray(drawn.astype(out[name].dtype))
    for name, factor in factors.items():
        out[name] = (out[name] * factor).astype(out[name].dtype)
    return out
```

```python
from contextlib import ExitStack

import concourse.bass as bass
from concourse import mybir

ALU = mybir.AluOpType
ACT = mybir.ActivationFunctionType
F32 = mybir.dt.float32
BF16 = mybir.dt.bfloat16
AX_X = mybir.AxisListType.X

P = 128
B = 16
T = 512
J = T // P
HU = 512
C = HU // P
NODES = 255
LEAVES = 256
NH = 16
DH = 8
RMS = 5
NQ = NH // 4
PARTS = 3
KROWS = PARTS * PARTS * DH
KALL = KROWS + PARTS
NE = 16
LN_EPS, RMS_EPS, K_EPS = 1e-5, 1e-6, 1e-8
K_CLAMP = 60.0
MASKED = -1e30

PER_BATCH = dict(
    x_loaded=16, ln_stats=8, ln_moments=8, ln_var=10, ln_rstd=8, ln0_hat=1, ln0_gain=1, x1_ready=1, pre_hat=1,
    xnT_ps=1, xnT=1, mix_diff=1, mixed=3, k_ps=4, v_ps=4, r_ps=4, k_exp=4, r_tanh=4, k_clamped=4, kv=4,
    k_sum=4, kv_sum=4, k_first=4, wk=4, wk_inv=4, wkv=4, gated=4, rwkv=4, wo_ps=1, woT=1, wo_tok_ps=1, x2_ready=1,
    residual=1, post_hat=1, xn2T_ps=1, xn2T=1, mix2_diff=1, mixed2=2, cmk_ps=4, cmk_tanh=4, silu=4, cmr_ps=1, cmr_tanh=1,
    cmv_ps=1, cmixT=1, cmix_tok_ps=1, y0=1, xb_ready=1,
    xbT_ps=1, xbT=1, gate_ps=2, gate_tanh=2, gate=1, leaf=15, leafT_ps=2, leafT=2, ffn_ps=1, ffnT=1, ffn_tok_ps=1,
    yb=1, xc_ready=1,
    xc_hat=1, xcT_ps=1, xcT=1, rope_ps=4, v_tok_ps=1, vaug=1, rope_mul=4, rope_out=2, part1=2, rest1=2, part2=2, part3=2,
    heads_in=16 * 2 * PARTS * PARTS, rowscore_ps=64, rowmax=64, maxT_ps=1, negmax=1, max_rest=1, max_parts=3, max_in=48,
    score_ps=20, prob=20, pv_ps=4, pvT=4, pv_tok_ps=4, pv_inv=4, attn=4,
    attnT_ps=1, attnT=1, proj_ps=1, yc=1, xd_ready=1,
    xdT_ps=1, xdT=1, logit_ps=1, logits=1, lmax=1, lshift=1, lexp=1, lsum=1, linv=1, prob_e=1, pick=9, hot=3, gates=1,
    gT_ps=1, gT=1, gb_ps=16, ug=16, moe_ps=1, moeT=1, moe_tok_ps=1, yd=1, out_ready=1, stored=16,
)


def build(nc: bass.Bass, a, out):
    with ExitStack() as ctx:
        def sb(name, shape, dt=F32):
            return ctx.enter_context(nc.sbuf_tensor(name, shape, dt))

        sems = {n: ctx.enter_context(nc.semaphore(f"s_{n}")) for n in PER_BATCH}
        setup = {n: ctx.enter_context(nc.semaphore(f"w_{n}")) for n in
                 ("loaded", "ident0", "ident", "consts", "scaled", "decay1", "decay", "turned_ps", "turned", "fused_ps", "fused", "rot", "ones")}

        passed = {e: ctx.enter_context(nc.semaphore(f"s_passed_{e.name}")) for e in (nc.sync.engine, nc.vector.engine, nc.gpsimd.engine)}

        def raised(ins, name, by=1):
            ins.then_inc(sems[name], by)

        def until(eng, b, name, n=None):
            per = PER_BATCH[name]
            eng.wait_ge(sems[name], b * per + (per if n is None else n))

        def apart(eng):
            eng.sem_inc(passed[eng.engine], 1)

        wk, wv, wr, cwk = (sb(n, [P, HU]) for n in ("wk", "wv", "wr", "cwk"))
        wo, cwv = (sb(n, [P, C, P]) for n in ("wo", "cwv"))
        cwr = sb("cwr", [P, P])
        vec_names = ["pre_g", "pre_b", "post_g", "post_b", "mix_k", "mix_v", "mix_r", "cmix_k", "cmix_r", "norm_scale", "wout_b"]
        vec = sb("vec", [P, len(vec_names)])
        v_ = {n: vec[:, i:i + 1] for i, n in enumerate(vec_names)}
        tdec, tfirst, dec_e, decay, first = (sb(n, [P, C]) for n in ("tdec", "tfirst", "dec_e", "decay", "first"))
        g0, b0 = sb("g0", [P, P]), sb("b0", [P, P])
        tq, wout = sb("tq", [P, P]), sb("wout", [P, P])
        routers, leaves = sb("routers", [P, 2, P]), sb("leaves", [P, 2, P])
        routersT, leavesT, woutT = sb("routersT", [P, LEAVES]), sb("leavesT", [P, LEAVES]), sb("woutT", [P, P])
        w_gate, w_leaf = sb("w_gate", [P, LEAVES]), sb("w_leaf", [P, 2, P])
        aq, ak, av, ao = (sb(n, [P, P]) for n in ("aq", "ak", "av", "ao"))
        w_rope = sb("w_rope", [P, 4, DH, NH])
        cos_t, sin_t = sb("cos_t", [P, T]), sb("sin_t", [P, T])
        cent, centT, ebias = sb("cent", [NE, P]), sb("centT", [P, NE]), sb("ebias", [P, NE])
        wexpT = sb("wexpT", [P, NE, P])
        prob = sb("prob", [P, 10, T])
        wexp = prob[:, 0:4, :].rearrange("p u (e h) -> p (u e) h", h=P)
        brow = sb("brow", [NE, P])
        wsh, wshs, wshT = sb("wsh", [P, 2, P]), sb("wshs", [P, P]), sb("wshT", [P, P])
        bsh, bshs = sb("bsh", [P, 2]), sb("bshs", [P, 1])
        ident, identb = sb("ident", [P, P]), sb("identb", [P, P], BF16)
        maskb, maskTb = sb("maskb", [P, P], BF16), sb("maskTb", [P, P], BF16)
        rank = sb("rank", [P, NE])
        exponent = sb("exponent", [P, J])
        keps = sb("keps", [P, 1])

        x0, x1, hat, x2, res = (sb(n, [P, J, P]) for n in ("x0", "x1", "hat", "x2", "res"))
        stats, mv, rstd = sb("stats", [P, 8, J, 6]), sb("mv", [P, 8, J, 2]), sb("rstd", [P, 8, J])
        var = sb("var", [P, 8, J])
        xnT, xn2T = sb("xnT", [P, T + 1]), sb("xn2T", [P, T + 1])
        dif = dif2 = sb("dif", [P, T])
        mixed = [sb(f"mixed{i}", [P, T]) for i in range(3)]
        mixed2 = mixed[0:2]
        kk, kvb, wkb, rth = (sb(n, [P, 2, T]) for n in ("kk", "kvb", "wkb", "rth"))
        inner = sb("inner", [P, C, T])
        ksum, kvsum = sb("ksum", [P, 2, T + 1]), sb("kvsum", [P, 2, T + 1])
        woT = sb("woT", [P, T])
        cth = sb("cth", [P, 2, T])
        rth2, cmT = sb("rth2", [P, T]), woT
        xb, xc = (sb(n, [P, J, P]) for n in ("xb", "xc"))
        y0, yb = x1, x2
        xbT = sb("xbT", [P, T])
        gate, lpa, lpb = (prob[:, u:u + 2, :].rearrange("p u (j n) -> p (u j) n", j=2) for u in (4, 6, 8))
        lpT = inner[:, 0:2, :]
        ffnT = woT
        xd, yo, att = (sb(n, [P, J, P]) for n in ("xd", "yo", "att"))
        xch, yc, yd = hat, res, att
        xcT = sb("xcT", [P, T])
        rope = [prob[:, i, :] for i in range(4)]
        qk = [sb(f"qk{i}", [P, T]) for i in range(2)]
        rest = [sb(f"rest{i}", [P, T]) for i in range(2)]
        part = [[sb(f"part{i}{j}", [P, T], BF16) for j in range(PARTS)] for i in range(2)]
        qh, kh = sb("qh", [KALL, NH, T], BF16), sb("kh", [KALL, NH, T], BF16)
        vaug = sb("vaug", [P, J, NH, 32])
        rmax = sb("rmax", [P, J, NH])
        nmax, mrest = sb("nmax", [NH, T]), sb("mrest", [NH, T])
        mpart = [sb(f"mpart{i}", [NH, T], BF16) for i in range(PARTS)]
        pvT = sb("pvT", [P, T])
        pvi = sb("pvi", [P, J, 4])
        attT = pvT
        xdT = xcT
        lg, lsh, lex, pe_, gts = (sb(n, [P, J, NE]) for n in ("lg", "lsh", "lex", "pe_", "gts"))
        lm, lsu, lin = (sb(n, [P, J]) for n in ("lm", "lsu", "lin"))
        eq1, key1, hot1, left, eq2, key2, hot2, hots = (sb(n, [P, J, NE]) for n in
            ("eq1", "key1", "hot1", "left", "eq2", "key2", "hot2", "hots"))
        m1, km1, m2, km2 = (sb(n, [P, J]) for n in ("m1", "km1", "m2", "km2"))
        gT = nmax
        ug = prob[:, 0:4, :]
        moT = pvT

        ps = [ctx.enter_context(nc.psum_tensor(f"bank{i}", [P, 1024], F32)) for i in range(4)]
        bank = [ps[i // 2][:, (i % 2) * 512:(i % 2) * 512 + 512] for i in range(8)]
        S, O, W = bank[0:4], bank[4], bank[5:8]
        SD = [ps[0], ps[1]]

        def tok(bk):
            return bk.rearrange("p (j h) -> p j h", j=J)

        def wide(t2, n):
            return t2.rearrange("p (j o) -> p j o", o=1).broadcast_to([P, J, n])

        block = ctx.enter_context(nc.Block())

        LOADS = [
            (wk[:, :], a["L0_attn_tm_Wk"]), (wv[:, :], a["L0_attn_tm_Wv"]), (wr[:, :], a["L0_attn_tm_Wr"]),
            (cwk[:, :], a["L0_attn_cm_Wk"]), (cwr[:, :], a["L0_attn_cm_Wr"]),
            (wo[:, :, :], a["L0_attn_tm_Wo"].rearrange("(c p) h -> p c h", p=P)),
            (cwv[:, :, :], a["L0_attn_cm_Wv"].rearrange("(c p) h -> p c h", p=P)),
            (tdec[:, :], a["L0_attn_tm_decay"].rearrange("(c p) -> p c", p=P)),
            (tfirst[:, :], a["L0_attn_tm_first"].rearrange("(c p) -> p c", p=P)),
            (g0[:, :], a["L0_attn_ln0_g"].rearrange("(o h) -> o h", o=1).broadcast_to([P, P])),
            (b0[:, :], a["L0_attn_ln0_b"].rearrange("(o h) -> o h", o=1).broadcast_to([P, P])),
            (tq[:, :], a["L0_ffn_Wq"]), (wout[:, :], a["L0_ffn_Wout_w"]),
            (routers[:, 0, :], a["L0_ffn_routers"][0:P, :]), (routers[0:NODES - P, 1, :], a["L0_ffn_routers"][P:NODES, :]),
            (leaves[:, :, :], a["L0_ffn_leaf_values"].rearrange("(k p) h -> p k h", p=P)),
            (aq[:, :], a["L1_attn_Wq"]), (ak[:, :], a["L1_attn_Wk"]), (av[:, :], a["L1_attn_Wv"]), (ao[:, :], a["L1_attn_Wo"]),
            (cos_t[:, :], a["rope_cos"]), (sin_t[:, :], a["rope_sin"]),
            (cent[:, :], a["L1_ffn_centroids"]),
            (ebias[:, :], a["L1_ffn_expert_biases"].rearrange("(o e) -> o e", o=1).broadcast_to([P, NE])),
            (wexp[:, :, :], a["L1_ffn_Wr"].rearrange("e o d -> o e d")), (brow[:, :], a["L1_ffn_br"]),
            (wsh[:, :, :], a["L1_ffn_Ws"].rearrange("n o d -> o n d")), (bsh[:, :], a["L1_ffn_bs"].rearrange("n o -> o n")),
        ]
        for n, src in (("pre_g", "L0_attn_pre_g"), ("pre_b", "L0_attn_pre_b"), ("post_g", "L0_attn_post_g"), ("post_b", "L0_attn_post_b"),
                       ("mix_k", "L0_attn_tm_mix_k"), ("mix_v", "L0_attn_tm_mix_v"), ("mix_r", "L0_attn_tm_mix_r"),
                       ("cmix_k", "L0_attn_cm_mix_k"), ("cmix_r", "L0_attn_cm_mix_r"), ("norm_scale", "L1_attn_norm_scale"),
                       ("wout_b", "L0_ffn_Wout_b")):
            LOADS.append((v_[n], a[src].rearrange("(p o) -> p o", o=1)))
        ALL_LOADED = 16 * len(LOADS)

        TURNS = [(routers[:, 0, :], P, routersT[:, 0:P]), (routers[0:NODES - P, 1, :], NODES - P, routersT[:, P:NODES]),
                 (leaves[:, 0, :], P, leavesT[:, 0:P]), (leaves[:, 1, :], P, leavesT[:, P:2 * P]),
                 (wout[:, :], P, woutT[:, :]), (cent[:, :], NE, centT[:, :]), (wshs[:, :], P, wshT[:, :])]
        TURNS += [(wexp[:, e, :], P, wexpT[:, e, :]) for e in range(NE)]

        @block.sync
        def _(sp):
            sp.dma_start(x0[:, :, :], a["L0_attn_x"][0].rearrange("(j p) h -> p j h", p=P)).then_inc(sems["x_loaded"], 16)
            for dst, src in LOADS:
                sp.dma_start(dst, src, allow_slow_non_contiguous=True).then_inc(setup["loaded"], 16)

            def batch(b, more):
                if more:
                    until(sp, b, "residual")
                    apart(sp)
                    src = a["L0_attn_x"][bass.ds(b + 1, 1)].rearrange("o (j p) h -> p (o j) h", p=P)
                    sp.dma_start(x0[:, :, :], src).then_inc(sems["x_loaded"], 16)
                for t, dst in enumerate((qh, kh)):
                    for m in range(PARTS):
                        until(sp, b, f"part{m + 1}", t + 1)
                        for o in range(PARTS):
                            r = (m * PARTS + o if t == 0 else o * PARTS + m) * DH
                            sp.dma_start(dst[r:r + DH, :, :], part[t][m][:, :]).then_inc(sems["heads_in"], 16)
                for i in range(PARTS):
                    until(sp, b, "max_parts", i + 1)
                    sp.dma_start(qh[KROWS + i:KROWS + i + 1, :, :], mpart[i][:, :]).then_inc(sems["max_in"], 16)
                until(sp, b, "out_ready")
                apart(sp)
                dst = out[bass.ds(b, 1)].rearrange("o (j p) h -> p (o j) h", p=P)
                sp.dma_start(dst, yo[:, :, :]).then_inc(sems["stored"], 16)
                until(sp, b, "stored")
                apart(sp)

            with sp.Fori(0, B - 1) as b:
                batch(b, True)
            batch(B - 1, False)

        @block.gpsimd
        def _(pool):
            pool.memset(ident[:, :], 0.0).then_inc(setup["ident0"], 1)
            pool.memset(identb[:, :], 0.0).then_inc(setup["ident0"], 1)
            pool.memset(maskTb[:, :], 0.0).then_inc(setup["ident0"], 1)
            pool.memset(maskb[:, :], 0.0).then_inc(setup["ident0"], 1)
            pool.memset(exponent[:, :], -0.5).then_inc(setup["ident0"], 1)
            pool.memset(keps[:, :], K_EPS).then_inc(setup["ident0"], 1)
            pool.memset(vaug[:, :, :, :], 0.0).then_inc(setup["ident0"], 1)
            pool.memset(kh[:, :, :], 1.0).then_inc(setup["ident0"], 1)
            pool.memset(ksum[:, :, 0:1], 0.0).then_inc(setup["ident0"], 1)
            pool.memset(kvsum[:, :, 0:1], 0.0).then_inc(setup["ident0"], 1)
            pool.memset(xnT[:, 0:1], 0.0).then_inc(setup["ident0"], 1)
            pool.memset(xn2T[:, 0:1], 0.0).then_inc(setup["ident0"], 1)
            pool.wait_ge(setup["ident0"], 12)
            pool.affine_select(out=ident[:, :], in_=ident[:, :], compare_op=ALU.not_equal, fill=1.0, base=0,
                               pattern=[[-1, P]], channel_multiplier=1).then_inc(setup["ident"], 1)
            pool.affine_select(out=identb[:, :], in_=identb[:, :], compare_op=ALU.not_equal, fill=1.0, base=0,
                               pattern=[[-1, P]], channel_multiplier=1).then_inc(setup["ident"], 1)
            pool.affine_select(out=maskb[:, :], in_=maskb[:, :], compare_op=ALU.is_ge, fill=MASKED, base=0,
                               pattern=[[-1, P]], channel_multiplier=1).then_inc(setup["ident"], 1)
            pool.affine_select(out=maskTb[:, :], in_=maskTb[:, :], compare_op=ALU.is_ge, fill=MASKED, base=0,
                               pattern=[[1, P]], channel_multiplier=-1).then_inc(setup["ident"], 1)
            pool.iota(rank[:, :], pattern=[[-1, NE]], base=NE, channel_multiplier=0,
                      allow_small_or_imprecise_dtypes=True).then_inc(setup["ident"], 1)
            pool.memset(vaug[:, :, :, DH:DH + 1], 1.0).then_inc(setup["ident"], 1)
            pool.wait_ge(setup["ident"], 6)

            def inverse_root(b, n, eps=LN_EPS, raw=False):
                until(pool, b, "ln_moments", n + 1)
                apart(pool)
                v = mv[:, n, :, 1]
                k = n + (2 if n > RMS else 0)
                if raw:
                    pool.tensor_tensor(rstd[:, n, :], mv[:, n, :, 0], mv[:, n, :, 0], ALU.mult).then_inc(sems["ln_var"], 1)
                    until(pool, b, "ln_var", n + 1)
                    pool.tensor_tensor(var[:, n, :], mv[:, n, :, 1], rstd[:, n, :], ALU.add).then_inc(sems["ln_var"], 1)
                    until(pool, b, "ln_var", n + 2)
                    apart(pool)
                    pool.tensor_scalar(var[:, n, :], var[:, n, :], eps, None, ALU.add).then_inc(sems["ln_var"], 1)
                    until(pool, b, "ln_var", n + 3)
                else:
                    pool.tensor_scalar(var[:, n, :], v, eps, None, ALU.add).then_inc(sems["ln_var"], 1)
                    until(pool, b, "ln_var", k + 1)
                pool.tensor_tensor(rstd[:, n, :], var[:, n, :], exponent[:, :], ALU.pow).then_inc(sems["ln_rstd"], 1)

            def over_tiles(t):
                return t.rearrange("p (o h) -> p o h", o=1).broadcast_to([P, J, P])

            pool.wait_ge(setup["loaded"], ALL_LOADED)
            with pool.Fori(0, B) as b:
                inverse_root(b, 0)
                until(pool, b, "ln0_hat")
                pool.tensor_tensor(hat[:, :, :], hat[:, :, :], over_tiles(g0[:, :]), ALU.mult).then_inc(sems["ln0_gain"], 1)
                until(pool, b, "ln0_gain")
                pool.tensor_tensor(x1[:, :, :], hat[:, :, :], over_tiles(b0[:, :]), ALU.add).then_inc(sems["x1_ready"], 1)
                inverse_root(b, 1)
                for c in range(C):
                    until(pool, b, "k_first", c + 1)
                    until(pool, b, "k_sum", c + 1)
                    pool.tensor_tensor(wkb[:, c % 2, :], wkb[:, c % 2, :], ksum[:, c % 2, 0:T], ALU.add).then_inc(sems["wk"], 1)
                    until(pool, b, "gated", c + 1)
                    pool.tensor_tensor(inner[:, c, :], rth[:, c % 2, :], wkb[:, c % 2, :], ALU.mult).then_inc(sems["rwkv"], 1)
                until(pool, b, "x2_ready")
                pool.tensor_tensor(res[:, :, :], x0[:, :, :], x2[:, :, :], ALU.add).then_inc(sems["residual"], 1)
                inverse_root(b, 2)
                inverse_root(b, 3)
                inverse_root(b, 4)
                inverse_root(b, 5, RMS_EPS, raw=True)
                for t in range(2):
                    until(pool, b, "rope_mul", 2 * t + 2)
                    pool.tensor_tensor(qk[t][:, :], rope[2 * t][:, :], rope[2 * t + 1][:, :], ALU.add).then_inc(sems["rope_out"], 1)
                for t in range(2):
                    until(pool, b, "part1", t + 1)
                    pool.tensor_tensor(rest[t][:, :], qk[t][:, :], part[t][0][:, :], ALU.subtract).then_inc(sems["rest1"], 1)
                for t in range(2):
                    until(pool, b, "part2", t + 1)
                    pool.tensor_tensor(part[t][2][:, :], rest[t][:, :], part[t][1][:, :], ALU.subtract).then_inc(sems["part3"], 1)
                inverse_root(b, 6)
                inverse_root(b, 7)

        @block.scalar
        def _(act):
            act.wait_ge(setup["loaded"], ALL_LOADED)
            act.wait_ge(setup["ident"], 6)
            act.activation(dec_e[:, :], tdec[:, :], ACT.Exp).then_inc(setup["decay1"], 1)
            act.activation(first[:, :], tfirst[:, :], ACT.Exp).then_inc(setup["decay1"], 1)
            act.wait_ge(setup["decay1"], 2)
            act.activation(decay[:, :], dec_e[:, :], ACT.Exp, scale=-1.0).then_inc(setup["decay"], 1)
            for n, (_, rows, dst) in enumerate(TURNS):
                act.wait_ge(setup["turned_ps"], n + 1)
                act.activation(dst, bank[n % 8][:, 0:rows], ACT.Copy).then_inc(setup["turned"], 1)
            act.wait_ge(setup["fused_ps"], 1)
            act.activation(w_gate[:, 0:NODES], bank[0][:, 0:NODES], ACT.Copy).then_inc(setup["fused"], 1)
            act.wait_ge(setup["fused_ps"], 2)
            act.activation(w_leaf[:, :, :], bank[1][:, 0:2 * P].rearrange("p (k h) -> p k h", k=2), ACT.Copy).then_inc(setup["fused"], 1)
            act.wait_ge(setup["rot"], 1)
            act.wait_ge(setup["fused"], 2)

            def move(b, dst, src, after, signal, n=None, **kw):
                until(act, b, after, n)
                raised(act.activation(dst, src, kw.pop("func", ACT.Identity), **kw), signal)

            with act.Fori(0, B) as b:
                move(b, xnT[:, 1:T + 1], W[0], "xnT_ps", "xnT", scale=v_["pre_g"], bias=v_["pre_b"])
                for c in range(C):
                    if c >= 2:
                        until(act, b, "rwkv", c - 1)
                    move(b, rth[:, c % 2, :], W[0], "r_ps", "r_tanh", c + 1, func=ACT.Tanh, scale=0.5)
                    move(b, kk[:, c % 2, :], kk[:, c % 2, :], "k_clamped", "k_exp", c + 1, func=ACT.Exp)
                    until(act, b, "k_exp", c + 1)
                    raised(act.activation(wkb[:, c % 2, :], kk[:, c % 2, :], ACT.Identity, scale=first[:, c:c + 1], bias=keps[:, 0:1]), "k_first")
                move(b, woT[:, :], W[1], "wo_ps", "woT")
                move(b, xn2T[:, 1:T + 1], W[0], "xn2T_ps", "xn2T", scale=v_["post_g"], bias=v_["post_b"])
                for c in range(C):
                    move(b, cth[:, c % 2, :], W[1 + c % 2], "cmk_ps", "cmk_tanh", c + 1, func=ACT.Tanh, scale=0.5)
                move(b, rth2[:, :], W[0], "cmr_ps", "cmr_tanh", func=ACT.Tanh, scale=0.5)
                move(b, xbT[:, :], W[0], "xbT_ps", "xbT")
                for k in range(2):
                    move(b, gate[:, 2 * k:2 * k + 2, 0:NODES], W[1 + k].rearrange("p (j n) -> p j n", j=2)[:, :, 0:NODES],
                         "gate_ps", "gate_tanh", k + 1, func=ACT.Tanh, scale=0.5)
                for k in range(2):
                    move(b, lpT[:, k, :], W[k], "leafT_ps", "leafT", k + 1)
                move(b, ffnT[:, :], W[2], "ffn_ps", "ffnT", bias=v_["wout_b"])
                move(b, xcT[:, :], S[0], "xcT_ps", "xcT", scale=v_["norm_scale"])
                move(b, vaug[:, :, :, 0:DH], tok(O).rearrange("p j (h d) -> p j h d", d=DH), "v_tok_ps", "vaug")
                for t in range(2):
                    move(b, part[t][0][:, :], qk[t][:, :], "rope_out", "part1", t + 1)
                for t in range(2):
                    move(b, part[t][1][:, :], rest[t][:, :], "rest1", "part2", t + 1)
                move(b, nmax[:, :], S[0][0:NH, :], "maxT_ps", "negmax", scale=-1.0)
                for g in range(NQ):
                    for u in range(5):
                        move(b, prob[:, 2 * u:2 * u + 2, :], SD[(5 * g + u) % 2][:, :].rearrange("p (u s) -> p u s", u=2),
                             "score_ps", "prob", 5 * g + u + 1, func=ACT.Exp, scale=float(DH) ** -0.5)
                    move(b, pvT[:, :], O, "pv_ps", "pvT", g + 1)
                move(b, attT[:, :], S[0], "attnT_ps", "attnT")
                move(b, xdT[:, :], S[0], "xdT_ps", "xdT")
                until(act, b, "lshift")
                raised(act.activation(lex[:, :, :], lsh[:, :, :], ACT.Exp), "lexp")
                move(b, gT[:, :], S[2][0:NE, :], "gT_ps", "gT")
                move(b, moT[:, :], O, "moe_ps", "moeT", bias=bshs[:, 0:1])

        @block.vector
        def _(dve):
            dve.wait_ge(setup["loaded"], ALL_LOADED)
            dve.tensor_scalar(wo[:, :, :], wo[:, :, :], 0.5, None, ALU.mult).then_inc(setup["scaled"], 1)
            dve.tensor_scalar(cwv[:, :, :], cwv[:, :, :], 0.5, None, ALU.mult).then_inc(setup["scaled"], 1)
            dve.tensor_tensor(wshs[:, :], wsh[:, 0, :], wsh[:, 1, :], ALU.add).then_inc(setup["scaled"], 1)
            dve.tensor_tensor(bshs[:, :], bsh[:, 0:1], bsh[:, 1:2], ALU.add).then_inc(setup["scaled"], 1)
            dve.wait_ge(setup["scaled"], 4)
            dve.tensor_scalar(wshs[:, :], wshs[:, :], 0.5, None, ALU.mult).then_inc(setup["scaled"], 1)
            dve.tensor_scalar(bshs[:, :], bshs[:, :], 0.5, None, ALU.mult).then_inc(setup["scaled"], 1)
            half = DH // 2
            for t, w in enumerate((aq, ak)):
                by_dim = w[:, :].rearrange("p (h d) -> p d h", d=DH)
                dve.tensor_copy(w_rope[:, 2 * t, :, :], by_dim)
                dve.tensor_scalar(w_rope[:, 2 * t + 1, 0:half, :], by_dim[:, half:DH, :], -1.0, None, ALU.mult)
                last = dve.tensor_copy(w_rope[:, 2 * t + 1, half:DH, :], by_dim[:, 0:half, :])
            last.then_inc(setup["rot"], 1)
            dve.wait_ge(setup["decay"], 1)
            dve.wait_ge(setup["rot"], 1)
            dve.wait_ge(setup["ident"], 6)

            def moments(b, n, t):
                for j in range(J):
                    last = dve.bn_stats(stats[:, n, j, :], t[:, j, :])
                raised(last, "ln_stats")
                until(dve, b, "ln_stats", n + 1)
                apart(dve)
                for j in range(J):
                    last = dve.bn_aggr(mv[:, n, j, :], stats[:, n, j, :])
                raised(last, "ln_moments")

            def norm(b, n, dst, t, signal, centred=True):
                until(dve, b, "ln_rstd", n + 1)
                for j in range(J):
                    if centred:
                        last = dve.tensor_scalar(dst[:, j, :], t[:, j, :], mv[:, n, j, 0:1], rstd[:, n, j:j + 1], ALU.subtract, ALU.mult)
                    else:
                        last = dve.tensor_scalar(dst[:, j, :], t[:, j, :], rstd[:, n, j:j + 1], None, ALU.mult)
                raised(last, signal)

            def clamp(b, c):
                until(dve, b, "k_ps", c + 1)
                if c >= 2:
                    until(dve, b, "k_first", c - 1)
                raised(dve.tensor_scalar(kk[:, c % 2, :], W[1], K_CLAMP, None, ALU.min), "k_clamped")

            def stt(out_, in0, scalar, in1, op0, op1):
                return dve.scalar_tensor_tensor(out=out_, in0=in0, scalar=scalar, in1=in1, op0=op0, op1=op1)

            with dve.Fori(0, B) as b:
                dve.wait_ge(sems["x_loaded"], b * 16 + 16)
                moments(b, 0, x0)
                norm(b, 0, hat, x0, "ln0_hat")
                until(dve, b, "x1_ready")
                moments(b, 1, x1)
                norm(b, 1, hat, x1, "pre_hat")
                until(dve, b, "xnT")
                raised(dve.tensor_tensor(dif[:, :], xnT[:, 1:T + 1], xnT[:, 0:T], ALU.subtract), "mix_diff")
                until(dve, b, "mix_diff")
                for i, m in enumerate(("mix_k", "mix_v", "mix_r")):
                    raised(stt(mixed[i][:, :], dif[:, :], v_[m], xnT[:, 0:T], ALU.mult, ALU.add), "mixed")
                for c in range(C):
                    if c == 0:
                        clamp(b, 0)
                    until(dve, b, "v_ps", c + 1)
                    until(dve, b, "k_exp", c + 1)
                    raised(dve.tensor_tensor(kvb[:, c % 2, :], kk[:, c % 2, :], W[2], ALU.mult), "kv")
                    dc = decay[:, c:c + 1].broadcast_to([P, T])
                    raised(dve.tensor_tensor_scan(ksum[:, c % 2, 1:T + 1], dc, kk[:, c % 2, :], 0.0, ALU.mult, ALU.add), "k_sum")
                    until(dve, b, "kv", c + 1)
                    raised(dve.tensor_tensor_scan(kvsum[:, c % 2, 1:T + 1], dc, kvb[:, c % 2, :], 0.0, ALU.mult, ALU.add), "kv_sum")
                    if c + 1 < C:
                        clamp(b, c + 1)
                    until(dve, b, "wk", c + 1)
                    raised(dve.reciprocal(wkb[:, c % 2, :], wkb[:, c % 2, :]), "wk_inv")
                    until(dve, b, "kv_sum", c + 1)
                    raised(stt(kvb[:, c % 2, :], kvb[:, c % 2, :], first[:, c:c + 1], kvsum[:, c % 2, 0:T], ALU.mult, ALU.add), "wkv")
                    until(dve, b, "wkv", c + 1)
                    until(dve, b, "r_tanh", c + 1)
                    raised(stt(rth[:, c % 2, :], rth[:, c % 2, :], 1.0, kvb[:, c % 2, :], ALU.add, ALU.mult), "gated")
                until(dve, b, "wo_tok_ps")
                raised(dve.tensor_tensor(x2[:, :, :], x1[:, :, :], tok(W[2]), ALU.add), "x2_ready")
                until(dve, b, "x2_ready")
                moments(b, 2, x2)
                norm(b, 2, hat, x2, "post_hat")
                until(dve, b, "xn2T")
                raised(dve.tensor_tensor(dif2[:, :], xn2T[:, 1:T + 1], xn2T[:, 0:T], ALU.subtract), "mix2_diff")
                until(dve, b, "mix2_diff")
                for i, m in enumerate(("cmix_k", "cmix_r")):
                    raised(stt(mixed2[i][:, :], dif2[:, :], v_[m], xn2T[:, 0:T], ALU.mult, ALU.add), "mixed2")
                for c in range(C):
                    until(dve, b, "cmk_tanh", c + 1)
                    raised(stt(inner[:, c, :], cth[:, c % 2, :], 1.0, W[1 + c % 2], ALU.add, ALU.mult), "silu")
                until(dve, b, "cmr_tanh")
                until(dve, b, "cmv_ps")
                raised(stt(cmT[:, :], rth2[:, :], 0.5, W[1], ALU.mult, ALU.add), "cmixT")
                until(dve, b, "cmix_tok_ps")
                until(dve, b, "residual")
                raised(stt(y0[:, :, :], tok(W[2]), 0.5, res[:, :, :], ALU.add, ALU.add), "y0")
                until(dve, b, "y0")
                moments(b, 3, y0)
                norm(b, 3, xb, y0, "xb_ready")
                until(dve, b, "gate_tanh")
                raised(dve.tensor_scalar(gate[:, :, 0:NODES], gate[:, :, 0:NODES], 0.5, 0.5, ALU.mult, ALU.add), "gate")
                until(dve, b, "gate")
                src, dst = lpa, lpb
                for level in range(8):
                    n = 2 ** level
                    g = gate[:, :, n - 1:2 * n - 1]
                    pair = dst[:, :, 0:2 * n].rearrange("p j (n s) -> p j n s", s=2)
                    if level == 0:
                        dve.tensor_copy(pair[:, :, :, 1], g)
                        raised(dve.tensor_scalar(pair[:, :, :, 0], g, -1.0, 1.0, ALU.mult, ALU.add), "leaf")
                    else:
                        raised(dve.tensor_tensor(pair[:, :, :, 1], src[:, :, 0:n], g, ALU.mult), "leaf")
                        until(dve, b, "leaf", 2 * level)
                        raised(dve.tensor_tensor(pair[:, :, :, 0], src[:, :, 0:n], pair[:, :, :, 1], ALU.subtract), "leaf")
                    until(dve, b, "leaf", 2 * level + 1)
                    src, dst = dst, src
                until(dve, b, "ffn_tok_ps")
                raised(dve.tensor_tensor(yb[:, :, :], xb[:, :, :], tok(W[0]), ALU.add), "yb")
                until(dve, b, "yb")
                moments(b, 4, yb)
                norm(b, 4, xc, yb, "xc_ready")
                until(dve, b, "xc_ready")
                moments(b, 5, xc)
                norm(b, 5, xch, xc, "xc_hat", centred=False)
                for i in range(4):
                    until(dve, b, "rope_ps", i + 1)
                    raised(dve.tensor_tensor(rope[i][:, :], (cos_t if i % 2 == 0 else sin_t)[:, :], S[(i + 1) % 4], ALU.mult), "rope_mul")
                for h in range(NH):
                    for j in range(J):
                        until(dve, b, "rowscore_ps", h * J + j + 1)
                        raised(dve.tensor_reduce(rmax[:, j, h:h + 1], S[j][:, 0:(j + 1) * P], AX_X, ALU.max), "rowmax")
                until(dve, b, "negmax")
                dve.tensor_copy(mpart[0][:, :], nmax[:, :]).then_inc(sems["max_parts"], 1)
                until(dve, b, "max_parts", 1)
                raised(dve.tensor_tensor(mrest[:, :], nmax[:, :], mpart[0][:, :], ALU.subtract), "max_rest")
                until(dve, b, "max_rest", 1)
                raised(dve.tensor_copy(mpart[1][:, :], mrest[:, :]), "max_parts")
                until(dve, b, "max_parts", 2)
                raised(dve.tensor_tensor(mpart[2][:, :], mrest[:, :], mpart[1][:, :], ALU.subtract), "max_parts")
                for g in range(NQ):
                    until(dve, b, "pv_tok_ps", g + 1)
                    o = tok(O).rearrange("p j (g r) -> p j g r", r=32)
                    raised(dve.reciprocal(pvi[:, :, :], o[:, :, :, DH]), "pv_inv")
                    until(dve, b, "pv_inv", g + 1)
                    raised(dve.tensor_tensor(att[:, :, :].rearrange("p j (h d) -> p j h d", d=DH)[:, :, 4 * g:4 * g + 4, :], o[:, :, :, 0:DH],
                                             pvi[:, :, :].rearrange("p j (g o) -> p j g o", o=1).broadcast_to([P, J, 4, DH]), ALU.mult), "attn")
                until(dve, b, "proj_ps")
                raised(dve.tensor_tensor(yc[:, :, :], xc[:, :, :], tok(S[1]), ALU.add), "yc")
                until(dve, b, "yc")
                moments(b, 6, yc)
                norm(b, 6, xd, yc, "xd_ready")
                until(dve, b, "logit_ps")
                ps_lg = S[1][:, 0:J * NE].rearrange("p (j e) -> p j e", j=J)
                raised(dve.tensor_tensor(lg[:, :, :], ps_lg, ebias[:, :].rearrange("p (o e) -> p o e", o=1).broadcast_to([P, J, NE]), ALU.add), "logits")
                until(dve, b, "logits")
                raised(dve.tensor_reduce(lm[:, :], lg[:, :, :], AX_X, ALU.max), "lmax")
                until(dve, b, "lmax")
                raised(dve.tensor_tensor(lsh[:, :, :], lg[:, :, :], wide(lm[:, :], NE), ALU.subtract), "lshift")
                until(dve, b, "lexp")
                raised(dve.tensor_reduce(lsu[:, :], lex[:, :, :], AX_X, ALU.add), "lsum")
                until(dve, b, "lsum")
                raised(dve.reciprocal(lin[:, :], lsu[:, :]), "linv")
                until(dve, b, "linv")
                raised(dve.tensor_tensor(pe_[:, :, :], lex[:, :, :], wide(lin[:, :], NE), ALU.mult), "prob_e")
                until(dve, b, "prob_e")
                ranks = rank[:, :].rearrange("p (o e) -> p o e", o=1).broadcast_to([P, J, NE])
                steps = iter(range(1, 10))

                def pick(ins):
                    raised(ins, "pick")
                    until(dve, b, "pick", next(steps))

                for s, m, eq, key, km, hot in ((pe_, m1, eq1, key1, km1, hot1), (left, m2, eq2, key2, km2, hot2)):
                    pick(dve.tensor_reduce(m[:, :], s[:, :, :], AX_X, ALU.max))
                    pick(dve.tensor_tensor(eq[:, :, :], s[:, :, :], wide(m[:, :], NE), ALU.is_equal))
                    pick(dve.tensor_tensor(key[:, :, :], eq[:, :, :], ranks, ALU.mult))
                    pick(dve.tensor_reduce(km[:, :], key[:, :, :], AX_X, ALU.max))
                    hotted = dve.tensor_tensor(hot[:, :, :], key[:, :, :], wide(km[:, :], NE), ALU.is_equal)
                    if s is pe_:
                        raised(hotted, "hot")
                        until(dve, b, "hot", 1)
                        pick(stt(left[:, :, :], hot1[:, :, :], -2.0, pe_[:, :, :], ALU.mult, ALU.add))
                raised(hotted, "hot")
                until(dve, b, "hot", 2)
                raised(dve.tensor_tensor(hots[:, :, :], hot1[:, :, :], hot2[:, :, :], ALU.add), "hot")
                until(dve, b, "hot", 3)
                raised(dve.tensor_tensor(gts[:, :, :], pe_[:, :, :], hots[:, :, :], ALU.mult), "gates")
                for e in range(NE):
                    until(dve, b, "gb_ps", e + 1)
                    raised(dve.tensor_tensor(ug[:, e % 4, :], xdT[:, :], S[e % 4], ALU.mult), "ug")
                until(dve, b, "moe_tok_ps")
                raised(stt(yd[:, :, :], xd[:, :, :], 2.0, tok(S[0]), ALU.mult, ALU.add), "yd")
                until(dve, b, "yd")
                moments(b, 7, yd)
                norm(b, 7, yo, yd, "out_ready")

        @block.tensor
        def _(pe):
            pe.wait_ge(setup["ident"], 6)
            pe.wait_ge(setup["loaded"], ALL_LOADED)
            pe.wait_ge(setup["scaled"], 6)
            pe.wait_ge(setup["rot"], 1)
            for n, (src, rows, _) in enumerate(TURNS):
                if n >= 8:
                    pe.wait_ge(setup["turned"], n - 7)
                pe.transpose(bank[n % 8][:, 0:rows], src, ident[0:rows, 0:rows]).then_inc(setup["turned_ps"], 1)
            pe.wait_ge(setup["turned"], len(TURNS))
            pe.matmul(bank[0][:, 0:NODES], tq[:, :], routersT[:, 0:NODES], start=True, stop=True).then_inc(setup["fused_ps"], 1)
            for k in range(2):
                last = pe.matmul(bank[1][:, k * P:(k + 1) * P], leavesT[:, k * P:(k + 1) * P], woutT[:, :], start=True, stop=True)
            last.then_inc(setup["fused_ps"], 1)
            pe.wait_ge(setup["fused"], 2)

            def turn(bk, t, signal):
                for j in range(J):
                    last = pe.transpose(bk[:, j * P:(j + 1) * P], t[:, j, :], ident[:, :])
                raised(last, signal)

            def mm(out_, w, x, start=True, stop=True, **kw):
                return pe.matmul(out_, w, x, start=start, stop=stop, **kw)

            def tiles(t):
                return t[:, :].rearrange("p (j h) -> p j h", j=J)

            with pe.Fori(0, B) as b:
                until(pe, b, "pre_hat")
                turn(W[0], hat, "xnT_ps")
                for c in range(C):
                    cs = slice(c * P, (c + 1) * P)
                    for i, (w, bk, done, freed) in enumerate(((wk, W[1], "k_ps", "k_clamped"), (wv, W[2], "v_ps", "kv"), (wr, W[0], "r_ps", "r_tanh"))):
                        until(pe, b, "mixed", i + 1) if c == 0 else until(pe, b, freed, c)
                        raised(mm(bk, w[:, cs], mixed[i][:, :]), done)
                until(pe, b, "k_clamped")
                for c in range(C):
                    until(pe, b, "rwkv", c + 1)
                    last = mm(W[1], wo[:, c, :], inner[:, c, :], c == 0, c == C - 1)
                raised(last, "wo_ps")
                until(pe, b, "woT")
                turn(W[2], tiles(woT), "wo_tok_ps")
                until(pe, b, "post_hat")
                turn(W[0], hat, "xn2T_ps")
                until(pe, b, "mixed2", 1)
                for c in range(C):
                    if c >= 2:
                        until(pe, b, "silu", c - 1)
                    raised(mm(W[1 + c % 2], cwk[:, c * P:(c + 1) * P], mixed2[0][:, :]), "cmk_ps")
                until(pe, b, "mixed2", 2)
                raised(mm(W[0], cwr[:, :], mixed2[1][:, :]), "cmr_ps")
                for c in range(C):
                    until(pe, b, "silu", max(c + 1, 3))
                    last = mm(W[1], cwv[:, c, :], inner[:, c, :], c == 0, c == C - 1)
                raised(last, "cmv_ps")
                until(pe, b, "cmixT")
                turn(W[2], tiles(cmT), "cmix_tok_ps")
                until(pe, b, "xb_ready")
                turn(W[0], xb, "xbT_ps")
                until(pe, b, "xbT")
                for k in range(2):
                    for j in range(2 * k, 2 * k + 2):
                        last = mm(W[1 + k][:, (j % 2) * LEAVES:(j % 2) * LEAVES + NODES], xbT[:, j * P:(j + 1) * P], w_gate[:, 0:NODES])
                    raised(last, "gate_ps")
                until(pe, b, "leaf")
                for k in range(2):
                    turn(W[k], lpa[:, :, k * P:(k + 1) * P], "leafT_ps")
                for k in range(2):
                    until(pe, b, "leafT", k + 1)
                    last = mm(W[2], w_leaf[:, k, :], lpT[:, k, :], k == 0, k == 1)
                raised(last, "ffn_ps")
                until(pe, b, "ffnT")
                turn(W[0], tiles(ffnT), "ffn_tok_ps")

                until(pe, b, "xc_hat")
                turn(S[0], xch, "xcT_ps")
                until(pe, b, "xcT")
                for i in range(4):
                    raised(mm(S[(i + 1) % 4], w_rope[:, i, :, :].rearrange("p d h -> p (d h)"), xcT[:, :]), "rope_ps")
                for j in range(J):
                    last = mm(O[:, j * P:(j + 1) * P], xcT[:, j * P:(j + 1) * P], av[:, :])
                raised(last, "v_tok_ps")
                until(pe, b, "rope_mul")
                until(pe, b, "heads_in")
                for h in range(NH):
                    for j in range(J):
                        n = h * J + j
                        if h:
                            until(pe, b, "rowmax", n - J + 1)
                        q = qh[0:KROWS, h, j * P:(j + 1) * P]
                        mm(S[j][:, 0:(j + 1) * P], q, kh[0:KROWS, h, 0:(j + 1) * P], True, False)
                        raised(mm(S[j][:, j * P:(j + 1) * P], identb[:, :], maskb[:, :], False, True), "rowscore_ps")
                until(pe, b, "rowmax")
                for j in range(J):
                    last = pe.transpose(S[0][0:NH, j * P:(j + 1) * P], rmax[:, j, :], ident[:, :])
                raised(last, "maxT_ps")
                until(pe, b, "negmax")
                until(pe, b, "max_in")

                def scores(bk, h, i, col):
                    mm(bk[:, col:col + T - i * P], kh[:, h, i * P:(i + 1) * P], qh[:, h, i * P:T], True, False, skip_group_check=True)
                    return mm(bk[:, col:col + P], identb[:, :], maskTb[:, :], False, True, skip_group_check=True)

                def weighted(g):
                    until(pe, b, "prob", 5 * g + 5)
                    until(pe, b, "vaug") if g == 0 else until(pe, b, "attn", g)
                    for i, unit in enumerate((lambda q: (q, 0), lambda q: (4 + q, 0), lambda q: (8 + q // 2, (q % 2) * 2 * P), lambda q: (4 + q, 3 * P))):
                        for q in range(4):
                            u, col = unit(q)
                            last = mm(O[32 * q:32 * q + 32, i * P:T], vaug[:, i, 4 * g + q, :], prob[:, u, col:col + T - i * P],
                                      i == 0, i == J - 1, tile_position=(0, 32 * q))
                    raised(last, "pv_ps")
                    until(pe, b, "pvT", g + 1)
                    turn(O, tiles(pvT), "pv_tok_ps")

                for g in range(NQ):
                    for u in range(5):
                        n = 5 * g + u
                        if n >= 2:
                            until(pe, b, "prob", n - 1)
                        for s in range(2):
                            bk = SD[n % 2][:, s * T:(s + 1) * T]
                            if u < 2:
                                last = scores(bk, 4 * g + 2 * u + s, 0, 0)
                            elif u < 4:
                                scores(bk, 4 * g + 2 * (u - 2) + s, 1, 0)
                                last = scores(bk, 4 * g + 2 * (u - 2) + s, 3, 3 * P)
                            else:
                                scores(bk, 4 * g + 2 * s, 2, 0)
                                last = scores(bk, 4 * g + 2 * s + 1, 2, 2 * P)
                        raised(last, "score_ps")
                    weighted(g)
                until(pe, b, "attn")
                until(pe, b, "prob")
                turn(S[0], att, "attnT_ps")
                until(pe, b, "attnT")
                for j in range(J):
                    last = mm(S[1][:, j * P:(j + 1) * P], attT[:, j * P:(j + 1) * P], ao[:, :])
                raised(last, "proj_ps")

                until(pe, b, "xd_ready")
                turn(S[0], xd, "xdT_ps")
                until(pe, b, "xdT")
                for j in range(J):
                    last = mm(S[1][:, j * NE:(j + 1) * NE], xdT[:, j * P:(j + 1) * P], centT[:, :])
                raised(last, "logit_ps")
                mm(O, wshT[:, :], xdT[:, :], True, False)
                until(pe, b, "gates")
                for j in range(J):
                    last = pe.transpose(S[2][0:NE, j * P:(j + 1) * P], gts[:, j, :], ident[:, :])
                raised(last, "gT_ps")
                until(pe, b, "gT")
                mm(O, brow[:, :], gT[:, :], False, False)

                def expert(e):
                    until(pe, b, "ug", e + 1)
                    return mm(O, wexpT[:, e, :], ug[:, e % 4, :], False, e == NE - 1)

                for e in range(NE):
                    if e >= 4:
                        until(pe, b, "ug", e - 3)
                    for j in range(J):
                        last = pe.transpose(S[e % 4][:, j * P:(j + 1) * P], gts[:, j, e:e + 1].broadcast_to([P, P]), ident[:, :])
                    raised(last, "gb_ps")
                    if e >= 2:
                        expert(e - 2)
                expert(NE - 2)
                raised(expert(NE - 1), "moe_ps")
                until(pe, b, "moeT")
                turn(S[0], tiles(moT), "moe_tok_ps")


_UNUSED = ["L0_ffn_leaf_keys"]
_ROPE_BASE = 1000000.0


def _rope_tables():
    import numpy as np
    half = DH // 2
    theta = (1.0 / np.power(np.float32(_ROPE_BASE), (2 * np.arange(half) / DH).astype(np.float32))).astype(np.float32)
    angles = (theta[:, None] * np.arange(T, dtype=np.float32)[None, :]).astype(np.float32)
    rows = np.repeat(np.tile(angles, (2, 1)), NH, axis=0)
    return np.cos(rows).astype(np.float32), np.sin(rows).astype(np.float32)


def kernel(**inputs):
    import numpy as _np
    import concourse.bacc as _bacc
    from concourse.bass_utils import run_bass_kernel_spmd as _run

    nc = _bacc.Bacc("TRN2", target_bir_lowering=False, num_devices=1)
    arrays, args = {}, {}
    given = {n: _np.ascontiguousarray(v) for n, v in inputs.items() if n not in _UNUSED}
    given["rope_cos"], given["rope_sin"] = _rope_tables()
    for name, v in given.items():
        arrays[f"in_{name}_dram"] = v
        args[name] = nc.dram_tensor(f"in_{name}_dram", v.shape, mybir.dt.from_np(v.dtype), kind="ExternalInput").ap()
    out = nc.dram_tensor("out_0_dram", (B, T, P), F32, kind="ExternalOutput").ap()
    build(nc, args, out)
    r = _run(nc, [arrays], core_ids=[0])
    return r.results[0]["out_0_dram"]
```

```python
from contextlib import ExitStack

import concourse.bass as bass
from concourse import mybir

ALU = mybir.AluOpType
ACT = mybir.ActivationFunctionType
F32 = mybir.dt.float32
BF16 = mybir.dt.bfloat16
AX_X = mybir.AxisListType.X

P = 128
B = 16
T = 512
J = T // P
HU = 512
C = HU // P
NODES = 255
LEAVES = 256
NH = 16
DH = 8
RMS = 5
NQ = NH // 4
PARTS = 3
KROWS = PARTS * PARTS * DH
KALL = KROWS + PARTS
NE = 16
LN_EPS, RMS_EPS, K_EPS = 1e-5, 1e-6, 1e-8
K_CLAMP = 60.0
MASKED = -1e30

PER_BATCH = dict(
    x_loaded=16, ln_stats=5, ln_moments=5, ln_var=5, ln_rstd=5, ln2_stats=1, ln2_moments=1, ln2_var=2, ln2_rstd=1,
    ln3_stats=2, ln3_moments=2, ln3_var=2, ln3_rstd=2, xc_kept=1, ln0_hat=1, ln0_gain=1, x1_ready=1, pre_hat=1,
    xnT_ps=1, xnT=1, mix_diff=1, mixed=3, k_ps=4, v_ps=4, r_ps=4, k_exp=4, r_tanh=4, k_clamped=4, kv=4,
    k_sum=4, kv_sum=4, k_first=4, wk=4, wk_inv=4, wkv=4, gated=4, rwkv=4, wo_ps=1, woT=1, wo_tok_ps=1, x2_ready=1,
    residual=1, post_hat=1, xn2T_ps=1, xn2T=1, mix2_diff=1, mixed2=2, cmk_ps=4, cmk_tanh=4, silu=4, cmr_ps=1, cmr_tanh=1,
    cmv_ps=1, cmixT=1, cmix_tok_ps=1, y0=1, xb_ready=1,
    xbT_ps=1, xbT=1, gate_ps=2, gate_tanh=2, gate=1, leaf=15, leafT_ps=2, leafT=2, ffn_ps=1, ffnT=1, ffn_tok_ps=1,
    yb=1, xc_ready=1,
    xc_hat=1, xcT_ps=1, xcT=1, rope_ps=4, v_tok_ps=1, vaug=1, rope_mul=4, rope_out=2, part1=2, rest1=2, part2=2, part3=2,
    heads_in=16 * 2 * PARTS * PARTS, rowscore_ps=64, rowmax=64, maxT_ps=1, negmax=1, max_rest=1, max_parts=3, max_in=48,
    score_ps=20, prob=20, pv_ps=12, pvT=4, pv_tok_ps=4, pv_inv=4, attn=4,
    attnT_ps=1, attnT=1, proj_ps=1, yc=1, xd_ready=1,
    xdT_ps=1, xdT=1, logit_ps=1, logits=1, lmax=1, lshift=1, lexp=1, lsum=1, linv=1, prob_e=1, pick=9, hot=3, gates=1,
    gate_part=4, gT_ps=1, gT=1, gb_ps=16, ug=16, moe_ps=1, moeT=1, moe_tok_ps=1, yd=1, out_ready=1, stored=16,
)


def build(nc: bass.Bass, a, out):
    with ExitStack() as ctx:
        def sb(name, shape, dt=F32):
            return ctx.enter_context(nc.sbuf_tensor(name, shape, dt))

        sems = {n: ctx.enter_context(nc.semaphore(f"s_{n}")) for n in PER_BATCH}
        setup = {n: ctx.enter_context(nc.semaphore(f"w_{n}")) for n in
                 ("loaded", "brow_parts", "ident0", "ident", "consts", "scaled", "decay1", "decay", "turned_ps", "turned", "fused_ps", "fused", "rot", "ones")}

        passed = {e: ctx.enter_context(nc.semaphore(f"s_passed_{e.name}")) for e in (nc.sync.engine, nc.vector.engine, nc.gpsimd.engine)}

        def raised(ins, name, by=1):
            ins.then_inc(sems[name], by)

        def until(eng, b, name, n=None):
            per = PER_BATCH[name]
            eng.wait_ge(sems[name], b * per + (per if n is None else n))

        def ln_of(n):
            return ("ln", n) if n < RMS else ("ln2", 0) if n == RMS else ("ln3", n - 6)

        def apart(eng):
            eng.sem_inc(passed[eng.engine], 1)

        wk, wv, wr, cwk = (sb(n, [P, HU]) for n in ("wk", "wv", "wr", "cwk"))
        wo, cwv = (sb(n, [P, C, P]) for n in ("wo", "cwv"))
        cwr = sb("cwr", [P, P])
        vec_names = ["pre_g", "pre_b", "post_g", "post_b", "mix_k", "mix_v", "mix_r", "cmix_k", "cmix_r", "norm_scale", "wout_b"]
        vec = sb("vec", [P, len(vec_names)])
        v_ = {n: vec[:, i:i + 1] for i, n in enumerate(vec_names)}
        tdec, tfirst, dec_e, decay, first = (sb(n, [P, C]) for n in ("tdec", "tfirst", "dec_e", "decay", "first"))
        g0, b0 = sb("g0", [P, P]), sb("b0", [P, P])
        w_gate, w_leaf = sb("w_gate", [P, LEAVES]), sb("w_leaf", [P, 2, P])
        aq, ak, av, ao = (sb(n, [P, P]) for n in ("aq", "ak", "av", "ao"))
        w_rope = sb("w_rope", [P, 4, DH, NH])
        cos_t, sin_t = sb("cos_t", [P, T]), sb("sin_t", [P, T])
        cent, centT, ebias = sb("cent", [NE, P]), sb("centT", [P, NE]), sb("ebias", [P, NE])
        wexpT = sb("wexpT", [P, NE, P])
        prob = sb("prob", [P, 10, T])
        came = prob[:, :, :].rearrange("p u (k h) -> p (u k) h", h=P)
        wexp, routers, leaves, wsh = came[:, 0:16, :], came[:, 16:18, :], came[:, 18:20, :], came[:, 20:22, :]
        tq, wout, wshs, woutT = (came[:, k, :] for k in (22, 23, 24, 25))
        routersT, leavesT = prob[:, 7, 0:LEAVES], prob[:, 7, LEAVES:2 * LEAVES]
        brow, brow_rest = sb("brow", [PARTS * NE, P]), sb("brow_rest", [PARTS * NE, P])
        brow_part = sb("brow_part", [PARTS * NE, PARTS, P], BF16)
        owner = sb("owner", [PARTS * NE, NE], BF16)
        wshT = sb("wshT", [P, P])
        bsh, bshs = sb("bsh", [P, 2]), sb("bshs", [P, 1])
        ident, identb = sb("ident", [P, P]), sb("identb", [P, P], BF16)
        maskb, maskTb = sb("maskb", [P, P], BF16), sb("maskTb", [P, P], BF16)
        rank = sb("rank", [P, NE])
        eps_ln, eps_rms = sb("eps_ln", [P, J]), sb("eps_rms", [P, J])
        exponent = sb("exponent", [P, J])
        keps = sb("keps", [P, 1])

        x0, x1, hat, x2, res = (sb(n, [P, J, P]) for n in ("x0", "x1", "hat", "x2", "res"))
        stats, mv, rstd = sb("stats", [P, 8, J, 6]), sb("mv", [P, 8, J, 2]), sb("rstd", [P, 8, J])
        var = sb("var", [P, 8, J])
        xnT, xn2T = sb("xnT", [P, T + 1]), sb("xn2T", [P, T + 1])
        dif = dif2 = sb("dif", [P, T])
        mixed = [sb(f"mixed{i}", [P, T]) for i in range(3)]
        mixed2 = mixed[0:2]
        kk, kvb, wkb, rth = (sb(n, [P, 2, T]) for n in ("kk", "kvb", "wkb", "rth"))
        inner = sb("inner", [P, C, T])
        ksum, kvsum = sb("ksum", [P, 2, T + 1]), sb("kvsum", [P, 2, T + 1])
        woT = sb("woT", [P, T])
        cth = sb("cth", [P, 2, T])
        rth2, cmT = sb("rth2", [P, T]), woT
        xb, xc = (sb(n, [P, J, P]) for n in ("xb", "xc"))
        y0, yb = x1, x2
        xbT = sb("xbT", [P, T])
        gate, lpa, lpb = (t[:, :, :].rearrange("p u (j n) -> p (u j) n", j=2) for t in (kk, kvb, rth))
        lpT = inner[:, 0:2, :]
        ffnT = woT
        kept = sb("kept", [P, J, P])
        xd, yo, att = (sb(n, [P, J, P]) for n in ("xd", "yo", "att"))
        xch, yc, yd = att, sb("yc", [P, J, P]), att
        xcT = sb("xcT", [P, T])
        rope = [prob[:, i, :] for i in range(4)]
        qk = [prob[:, 4 + i, :] for i in range(2)]
        rest = [prob[:, 6 + i, :] for i in range(2)]
        part = [[sb(f"part{i}{j}", [P, T], BF16) for j in range(PARTS)] for i in range(2)]
        qh, kh = sb("qh", [KALL, NH, T], BF16), sb("kh", [KALL, NH, T], BF16)
        vaug = sb("vaug", [P, J, NH, 32])
        rmax = sb("rmax", [P, J, NH])
        nmax, mrest = sb("nmax", [NH, T]), sb("mrest", [NH, T])
        mpart = [sb(f"mpart{i}", [NH, T], BF16) for i in range(PARTS)]
        pvT = sb("pvT", [P, T])
        pvi = sb("pvi", [P, J, 4])
        attT = pvT
        xdT = sb("xdT", [P, T])
        lg, lsh, lex, pe_, gts = (sb(n, [P, J, NE]) for n in ("lg", "lsh", "lex", "pe_", "gts"))
        lm, lsu, lin = (sb(n, [P, J]) for n in ("lm", "lsu", "lin"))
        eq1, key1, hot1, left, eq2, key2, hot2, hots = (sb(n, [P, J, NE]) for n in
            ("eq1", "key1", "hot1", "left", "eq2", "key2", "hot2", "hots"))
        m1, km1, m2, km2 = (sb(n, [P, J]) for n in ("m1", "km1", "m2", "km2"))
        gate_part, gate_rest = sb("gate_part", [P, J, PARTS, NE], BF16), sb("gate_rest", [P, J, NE])
        gT = sb("gT", [PARTS * NE, T], BF16)
        ug = prob[:, 0:4, :]
        moT = pvT

        ps = [ctx.enter_context(nc.psum_tensor(f"bank{i}", [P, 1024], F32)) for i in range(4)]
        bank = [ps[i // 2][:, (i % 2) * 512:(i % 2) * 512 + 512] for i in range(8)]
        S, O, W = bank[0:4], bank[4], bank[5:8]
        SD = [ps[0], ps[1]]

        def tok(bk):
            return bk.rearrange("p (j h) -> p j h", j=J)

        def wide(t2, n):
            return t2.rearrange("p (j o) -> p j o", o=1).broadcast_to([P, J, n])

        TILE_ORDER = (3, 0, 2, 1)

        def row_place(j):
            bk, col = {3: (S[0], 0), 0: (S[2], 0), 2: (S[2], P), 1: (S[1], 0)}[j]
            return bk[:, col:col + (j + 1) * P]

        block = ctx.enter_context(nc.Block())

        LOADS = [
            (wk[:, :], a["L0_attn_tm_Wk"]), (wv[:, :], a["L0_attn_tm_Wv"]), (wr[:, :], a["L0_attn_tm_Wr"]),
            (cwk[:, :], a["L0_attn_cm_Wk"]), (cwr[:, :], a["L0_attn_cm_Wr"]),
            (wo[:, :, :], a["L0_attn_tm_Wo"].rearrange("(c p) h -> p c h", p=P)),
            (cwv[:, :, :], a["L0_attn_cm_Wv"].rearrange("(c p) h -> p c h", p=P)),
            (tdec[:, :], a["L0_attn_tm_decay"].rearrange("(c p) -> p c", p=P)),
            (tfirst[:, :], a["L0_attn_tm_first"].rearrange("(c p) -> p c", p=P)),
            (g0[:, :], a["L0_attn_ln0_g"].rearrange("(o h) -> o h", o=1).broadcast_to([P, P])),
            (b0[:, :], a["L0_attn_ln0_b"].rearrange("(o h) -> o h", o=1).broadcast_to([P, P])),
            (tq[:, :], a["L0_ffn_Wq"]), (wout[:, :], a["L0_ffn_Wout_w"]),
            (routers[:, 0, :], a["L0_ffn_routers"][0:P, :]), (routers[0:NODES - P, 1, :], a["L0_ffn_routers"][P:NODES, :]),
            (leaves[:, :, :], a["L0_ffn_leaf_values"].rearrange("(k p) h -> p k h", p=P)),
            (aq[:, :], a["L1_attn_Wq"]), (ak[:, :], a["L1_attn_Wk"]), (av[:, :], a["L1_attn_Wv"]), (ao[:, :], a["L1_attn_Wo"]),
            (cos_t[:, :], a["rope_cos"]), (sin_t[:, :], a["rope_sin"]),
            (cent[:, :], a["L1_ffn_centroids"]),
            (ebias[:, :], a["L1_ffn_expert_biases"].rearrange("(o e) -> o e", o=1).broadcast_to([P, NE])),
            (wexp[:, :, :], a["L1_ffn_Wr"].rearrange("e o d -> o e d")), *((brow[i * NE:(i + 1) * NE, :], a["L1_ffn_br"]) for i in range(PARTS)),
            (wsh[:, :, :], a["L1_ffn_Ws"].rearrange("n o d -> o n d")), (bsh[:, :], a["L1_ffn_bs"].rearrange("n o -> o n")),
        ]
        for n, src in (("pre_g", "L0_attn_pre_g"), ("pre_b", "L0_attn_pre_b"), ("post_g", "L0_attn_post_g"), ("post_b", "L0_attn_post_b"),
                       ("mix_k", "L0_attn_tm_mix_k"), ("mix_v", "L0_attn_tm_mix_v"), ("mix_r", "L0_attn_tm_mix_r"),
                       ("cmix_k", "L0_attn_cm_mix_k"), ("cmix_r", "L0_attn_cm_mix_r"), ("norm_scale", "L1_attn_norm_scale"),
                       ("wout_b", "L0_ffn_Wout_b")):
            LOADS.append((v_[n], a[src].rearrange("(p o) -> p o", o=1)))
        ALL_LOADED = 16 * len(LOADS)

        TURNS = [(routers[:, 0, :], P, routersT[:, 0:P]), (routers[0:NODES - P, 1, :], NODES - P, routersT[:, P:NODES]),
                 (leaves[:, 0, :], P, leavesT[:, 0:P]), (leaves[:, 1, :], P, leavesT[:, P:2 * P]),
                 (wout[:, :], P, woutT[:, :]), (cent[:, :], NE, centT[:, :]), (wshs[:, :], P, wshT[:, :])]
        TURNS += [(wexp[:, e, :], P, wexpT[:, e, :]) for e in range(NE)]

        ORDER = """
            e:score0 t:moments0 t:norm0 e:score1 t:moments1 e:score2 e:score3 t:norm1 e:score4 e:score5 e:score6
            e:weigh0 e:back0 t:turn_pre e:score7 t:mix e:score8 e:score9 t:project0 t:clamp0 t:sums0 a:moments5
            t:read0 t:clamp1 e:score10 e:score11 e:weigh1 e:score12 e:score13 t:project1 e:back1 t:sums1 t:read1
            t:clamp2 e:score14 e:score15 t:project2 e:score16 e:weigh2 t:sums2 t:clamp3 e:score17 t:project3
            e:back2 e:score18 e:score19 e:weigh3 t:read2 t:sums3 e:back3 e:project t:read3 e:moments6 t:read_out
            a:norm5 e:norm6 e:turn_experts t:moments2 e:route a:turn_in t:norm2 a:rope e:turn_gates t:turn_post
            t:mix2 a:values_out e:start_experts a:parts e:expert0 t:channel_in t:channel_out t:moments3 e:expert1 a:rowmax0
            e:expert2 t:norm3 a:rowmax1 e:expert3 a:rowmax2 e:expert4 a:rowmax3 t:turn_tree e:expert5 a:rowmax4
            e:expert6 a:rowmax5 a:rowmax6 e:expert7 a:rowmax7 e:expert8 a:rowmax8 e:expert9 a:rowmax9 t:gates
            a:rowmax10 e:expert10 a:rowmax11 e:expert11 a:rowmax12 e:expert12 a:rowmax13 e:expert13 a:rowmax14
            e:expert14 a:rowmax15 e:expert15 e:experts_out t:tree a:maxima e:moments7 t:leaves t:moments4 e:norm7
            t:norm4 e:o_free
        """.split()

        def run(steps, b_t, b_a, b_e):
            for name in ORDER:
                b = {"t": b_t, "a": b_a, "e": b_e}[name[0]]
                if b is not None and name[2:] in steps:
                    steps[name[2:]](b)

        def turns(eng, steps):
            run(steps, 0, None, None)
            run(steps, 1, 0, None)
            with eng.Fori(2, B) as b:
                run(steps, b, b - 1, b - 2)
            run(steps, None, B - 1, B - 2)
            run(steps, None, None, B - 1)

        def each(name, n, f):
            return {f"{name}{k}": (lambda b, k=k: f(b, k)) for k in range(n)}

        @block.sync
        def _(sp):
            sp.dma_start(x0[:, :, :], a["L0_attn_x"][0].rearrange("(j p) h -> p j h", p=P)).then_inc(sems["x_loaded"], 16)
            for dst, src in LOADS:
                sp.dma_start(dst, src, allow_slow_non_contiguous=True).then_inc(setup["loaded"], 16)

            def load_next(b):
                until(sp, b, "residual")
                apart(sp)
                src = a["L0_attn_x"][bass.ds(b + 1, 1)].rearrange("o (j p) h -> p (o j) h", p=P)
                sp.dma_start(x0[:, :, :], src).then_inc(sems["x_loaded"], 16)

            def spread_heads(b):
                for t, dst in enumerate((qh, kh)):
                    for m in range(PARTS):
                        until(sp, b, f"part{m + 1}", t + 1)
                        for o in range(PARTS):
                            r = (m * PARTS + o if t == 0 else o * PARTS + m) * DH
                            sp.dma_start(dst[r:r + DH, :, :], part[t][m][:, :]).then_inc(sems["heads_in"], 16)

            def spread_maxima(b):
                for i in range(PARTS):
                    until(sp, b, "max_parts", i + 1)
                    sp.dma_start(qh[KROWS + i:KROWS + i + 1, :, :], mpart[i][:, :]).then_inc(sems["max_in"], 16)

            def store(b):
                until(sp, b, "out_ready")
                apart(sp)
                dst = out[bass.ds(b, 1)].rearrange("o (j p) h -> p (o j) h", p=P)
                sp.dma_start(dst, yo[:, :, :]).then_inc(sems["stored"], 16)
                apart(sp)
                until(sp, b, "stored")
                apart(sp)

            load_next(0)
            load_next(1)
            spread_heads(0)
            spread_maxima(0)
            with sp.Fori(2, B - 1) as b:
                load_next(b)
                spread_heads(b - 1)
                spread_maxima(b - 1)
                store(b - 2)
            for b in (B - 1, B):
                spread_heads(b - 1)
                spread_maxima(b - 1)
                store(b - 2)
            store(B - 1)

        @block.gpsimd
        def _(pool):
            zeroed = (ident[:, :], identb[:, :], maskb[:, :], maskTb[:, :], vaug[:, :, :, :], ksum[:, :, 0:1], kvsum[:, :, 0:1],
                      xnT[:, 0:1], xn2T[:, 0:1])
            filled = ((exponent[:, :], -0.5), (eps_ln[:, :], LN_EPS), (eps_rms[:, :], RMS_EPS), (keps[:, :], K_EPS), (kh[:, :, :], 1.0))
            for t, value in (*((z, 0.0) for z in zeroed), *filled):
                pool.memset(t, value).then_inc(setup["ident0"], 1)
            pool.wait_ge(setup["ident0"], len(zeroed) + len(filled))
            for t, op, fill, step in ((ident, ALU.not_equal, 1.0, -1), (identb, ALU.not_equal, 1.0, -1),
                                      (maskb, ALU.is_ge, MASKED, -1),
                                      (maskTb, ALU.is_ge, MASKED, 1)):
                pool.affine_select(out=t[:, :], in_=t[:, :], compare_op=op, fill=fill, base=0,
                                   pattern=[[step, P]], channel_multiplier=-step).then_inc(setup["ident"], 1)
            pool.iota(rank[:, :], pattern=[[-1, NE]], base=NE, channel_multiplier=0,
                      allow_small_or_imprecise_dtypes=True).then_inc(setup["ident"], 1)
            pool.memset(vaug[:, :, :, DH:DH + 1], 1.0).then_inc(setup["ident"], 1)
            pool.wait_ge(setup["ident"], 6)

            def inverse_root(b, n):
                ln, k = ln_of(n)
                until(pool, b, f"{ln}_moments", k + 1)
                raised(pool.tensor_tensor(var[:, n, :], mv[:, n, :, 1], eps_ln[:, :], ALU.add), f"{ln}_var")
                until(pool, b, f"{ln}_var", k + 1)
                raised(pool.tensor_tensor(rstd[:, n, :], var[:, n, :], exponent[:, :], ALU.pow), f"{ln}_rstd")

            def inverse_rms(b):
                until(pool, b, "ln2_moments", 1)
                pool.tensor_tensor(var[:, RMS, :], mv[:, RMS, :, 1], eps_rms[:, :], ALU.add)
                raised(pool.tensor_tensor(rstd[:, RMS, :], mv[:, RMS, :, 0], mv[:, RMS, :, 0], ALU.mult), "ln2_var")
                until(pool, b, "ln2_var", 1)
                raised(pool.tensor_tensor(mv[:, RMS, :, 1], var[:, RMS, :], rstd[:, RMS, :], ALU.add), "ln2_var")
                until(pool, b, "ln2_var", 2)
                raised(pool.tensor_tensor(rstd[:, RMS, :], mv[:, RMS, :, 1], exponent[:, :], ALU.pow), "ln2_rstd")

            def over_tiles(t):
                return t.rearrange("p (o h) -> p o h", o=1).broadcast_to([P, J, P])

            def first_gain(b):
                until(pool, b, "ln0_hat")
                raised(pool.tensor_tensor(hat[:, :, :], hat[:, :, :], over_tiles(g0[:, :]), ALU.mult), "ln0_gain")
                until(pool, b, "ln0_gain")
                raised(pool.tensor_tensor(x1[:, :, :], hat[:, :, :], over_tiles(b0[:, :]), ALU.add), "x1_ready")

            def rope_sum(b):
                for t in range(2):
                    until(pool, b, "rope_mul", 2 * t + 2)
                    raised(pool.tensor_tensor(qk[t], rope[2 * t], rope[2 * t + 1], ALU.add), "rope_out")

            def parts(b):
                for t in range(2):
                    until(pool, b, "part1", t + 1)
                    raised(pool.tensor_tensor(rest[t], qk[t], part[t][0][:, :], ALU.subtract), "rest1")
                for t in range(2):
                    until(pool, b, "part2", t + 1)
                    raised(pool.tensor_tensor(part[t][2][:, :], rest[t], part[t][1][:, :], ALU.subtract), "part3")

            def read(b, c):
                until(pool, b, "k_first", c + 1)
                until(pool, b, "k_sum", c + 1)
                raised(pool.tensor_tensor(wkb[:, c % 2, :], wkb[:, c % 2, :], ksum[:, c % 2, 0:T], ALU.add), "wk")
                until(pool, b, "gated", c + 1)
                raised(pool.tensor_tensor(inner[:, c, :], rth[:, c % 2, :], wkb[:, c % 2, :], ALU.mult), "rwkv")

            def residual(b):
                until(pool, b, "x2_ready")
                raised(pool.tensor_tensor(res[:, :, :], x0[:, :, :], x2[:, :, :], ALU.add), "residual")

            pool.wait_ge(setup["loaded"], ALL_LOADED)
            turns(pool, {
                **{f"norm{n}": (lambda b, n=n: inverse_root(b, n)) for n in (1, 2, 3, 4, 6, 7)},
                "norm0": lambda b: (inverse_root(b, 0), first_gain(b)), "norm5": inverse_rms,
                "rope": rope_sum, "parts": parts, **each("read", C, read), "moments2": residual,
            })

        @block.scalar
        def _(act):
            act.wait_ge(setup["loaded"], ALL_LOADED)
            act.wait_ge(setup["ident"], 6)
            act.activation(dec_e[:, :], tdec[:, :], ACT.Exp).then_inc(setup["decay1"], 1)
            act.activation(first[:, :], tfirst[:, :], ACT.Exp).then_inc(setup["decay1"], 1)
            act.wait_ge(setup["decay1"], 2)
            act.activation(decay[:, :], dec_e[:, :], ACT.Exp, scale=-1.0).then_inc(setup["decay"], 1)
            for n, (_, rows, dst) in enumerate(TURNS):
                act.wait_ge(setup["turned_ps"], n + 1)
                act.activation(dst, bank[n % 8][:, 0:rows], ACT.Copy).then_inc(setup["turned"], 1)
            act.wait_ge(setup["fused_ps"], 1)
            act.activation(w_gate[:, 0:NODES], bank[0][:, 0:NODES], ACT.Copy).then_inc(setup["fused"], 1)
            act.wait_ge(setup["fused_ps"], 2)
            act.activation(w_leaf[:, :, :], bank[1][:, 0:2 * P].rearrange("p (k h) -> p k h", k=2), ACT.Copy).then_inc(setup["fused"], 1)
            act.wait_ge(setup["rot"], 1)
            act.wait_ge(setup["fused"], 2)

            def move(b, dst, src, after, signal, n=None, func=ACT.Identity, **kw):
                until(act, b, after, n)
                raised(act.activation(dst, src, func, **kw), signal)

            def turn_pre(b):
                move(b, xnT[:, 1:T + 1], W[0], "xnT_ps", "xnT", scale=v_["pre_g"], bias=v_["pre_b"])

            def sums(b, c):
                if c >= 2:
                    until(act, b, "rwkv", c - 1)
                move(b, rth[:, c % 2, :], W[0], "r_ps", "r_tanh", c + 1, func=ACT.Tanh, scale=0.5)
                move(b, kk[:, c % 2, :], kk[:, c % 2, :], "k_clamped", "k_exp", c + 1, func=ACT.Exp)
                until(act, b, "k_exp", c + 1)
                raised(act.activation(wkb[:, c % 2, :], kk[:, c % 2, :], ACT.Identity, scale=first[:, c:c + 1], bias=keps[:, 0:1]), "k_first")

            def channel_in(b):
                for c in range(C):
                    if c >= 2:
                        until(act, b, "silu", c - 1)
                    move(b, cth[:, c % 2, :], W[1 + c % 2], "cmk_ps", "cmk_tanh", c + 1, func=ACT.Tanh, scale=0.5)
                move(b, rth2[:, :], W[0], "cmr_ps", "cmr_tanh", func=ACT.Tanh, scale=0.5)

            def gates(b):
                for k in range(2):
                    move(b, gate[:, 2 * k:2 * k + 2, 0:NODES], W[1 + k].rearrange("p (j n) -> p j n", j=2)[:, :, 0:NODES],
                         "gate_ps", "gate_tanh", k + 1, func=ACT.Tanh, scale=0.5)

            def leaves_out(b):
                for k in range(2):
                    move(b, lpT[:, k, :], W[k], "leafT_ps", "leafT", k + 1)
                move(b, ffnT[:, :], W[2], "ffn_ps", "ffnT", bias=v_["wout_b"])

            def rope_values(b):
                move(b, vaug[:, :, :, 0:DH], tok(O).rearrange("p j (h d) -> p j h d", d=DH), "v_tok_ps", "vaug")

            def parts(b):
                move(b, kept[:, :, :], xc[:, :, :], "rope_out", "xc_kept")
                until(act, b, "rope_out")
                for t in range(2):
                    raised(act.activation(part[t][0][:, :], qk[t], ACT.Identity), "part1")
                for t in range(2):
                    move(b, part[t][1][:, :], rest[t], "rest1", "part2", t + 1)

            def score(b, n):
                g, u = n // 5, n % 5
                if g:
                    until(act, b, "pv_ps", 3 * g - 2 + (0, 0, 1, 1, 2)[u])
                move(b, prob[:, 2 * u:2 * u + 2, :], SD[n % 2][:, :].rearrange("p (u s) -> p u s", u=2),
                     "score_ps", "prob", n + 1, func=ACT.Exp, scale=float(DH) ** -0.5)

            def expert_weights(b):
                until(act, b, "lshift")
                raised(act.activation(lex[:, :, :], lsh[:, :, :], ACT.Exp), "lexp")

            turns(act, {
                "turn_pre": turn_pre, **each("sums", C, sums), "read_out": lambda b: move(b, woT[:, :], W[1], "wo_ps", "woT"),
                "turn_post": lambda b: move(b, xn2T[:, 1:T + 1], W[0], "xn2T_ps", "xn2T", scale=v_["post_g"], bias=v_["post_b"]),
                "channel_in": channel_in, "turn_tree": lambda b: move(b, xbT[:, :], W[0], "xbT_ps", "xbT"),
                "gates": gates, "leaves": leaves_out,
                "turn_in": lambda b: move(b, xcT[:, :], S[0], "xcT_ps", "xcT", scale=v_["norm_scale"]),
                "rope": rope_values, "parts": parts,
                "maxima": lambda b: move(b, nmax[:, :], S[0][0:NH, :], "maxT_ps", "negmax", scale=-1.0),
                **each("score", 5 * NQ, score), **each("back", NQ, lambda b, g: move(b, pvT[:, :], O, "pv_ps", "pvT", 3 * g + 3)),
                "project": lambda b: move(b, attT[:, :], S[3], "attnT_ps", "attnT"),
                "turn_experts": lambda b: move(b, xdT[:, :], S[3], "xdT_ps", "xdT"),
                "route": expert_weights, "turn_gates": lambda b: move(b, gT[:, :], S[3][0:PARTS * NE, :], "gT_ps", "gT"),
                "experts_out": lambda b: move(b, moT[:, :], O, "moe_ps", "moeT", bias=bshs[:, 0:1]),
            })

        @block.vector
        def _(dve):
            dve.wait_ge(setup["loaded"], ALL_LOADED)
            dve.tensor_scalar(wo[:, :, :], wo[:, :, :], 0.5, None, ALU.mult).then_inc(setup["scaled"], 1)
            dve.tensor_scalar(cwv[:, :, :], cwv[:, :, :], 0.5, None, ALU.mult).then_inc(setup["scaled"], 1)
            dve.tensor_tensor(wshs, wsh[:, 0, :], wsh[:, 1, :], ALU.add).then_inc(setup["scaled"], 1)
            dve.tensor_tensor(bshs[:, :], bsh[:, 0:1], bsh[:, 1:2], ALU.add).then_inc(setup["scaled"], 1)
            dve.wait_ge(setup["scaled"], 4)
            dve.tensor_scalar(wshs, wshs, 0.5, None, ALU.mult).then_inc(setup["scaled"], 1)
            dve.tensor_scalar(bshs[:, :], bshs[:, :], 0.5, None, ALU.mult).then_inc(setup["scaled"], 1)
            half = DH // 2
            for t, w in enumerate((aq, ak)):
                by_dim = w[:, :].rearrange("p (h d) -> p d h", d=DH)
                dve.tensor_copy(w_rope[:, 2 * t, :, :], by_dim)
                dve.tensor_scalar(w_rope[:, 2 * t + 1, 0:half, :], by_dim[:, half:DH, :], -1.0, None, ALU.mult)
                last = dve.tensor_copy(w_rope[:, 2 * t + 1, half:DH, :], by_dim[:, 0:half, :])
            last.then_inc(setup["rot"], 1)
            def after_steps(n):
                dve.wait_ge(setup["brow_parts"], n)
            dve.tensor_copy(brow_part[:, 0, :], brow[:, :]).then_inc(setup["brow_parts"], 1)
            after_steps(1)
            dve.tensor_tensor(brow_rest[:, :], brow[:, :], brow_part[:, 0, :], ALU.subtract).then_inc(setup["brow_parts"], 1)
            after_steps(2)
            dve.tensor_copy(brow_part[:, 1, :], brow_rest[:, :]).then_inc(setup["brow_parts"], 1)
            after_steps(3)
            dve.tensor_tensor(brow_part[:, 2, :], brow_rest[:, :], brow_part[:, 1, :], ALU.subtract).then_inc(setup["brow_parts"], 1)
            after_steps(4)
            dve.wait_ge(setup["ident"], 6)
            dve.tensor_tensor(brow_rest[:, 0:NE], ident[0:PARTS * NE, 0:NE], ident[0:PARTS * NE, NE:2 * NE], ALU.add).then_inc(setup["brow_parts"], 1)
            after_steps(5)
            dve.tensor_tensor(owner[:, :], brow_rest[:, 0:NE], ident[0:PARTS * NE, 2 * NE:3 * NE], ALU.add).then_inc(setup["brow_parts"], 1)
            dve.wait_ge(setup["decay"], 1)
            dve.wait_ge(setup["rot"], 1)
            dve.wait_ge(setup["ident"], 6)

            def moments(b, n, t):
                ln, k = ln_of(n)
                for j in range(J):
                    last = dve.bn_stats(stats[:, n, j, :], t[:, j, :])
                raised(last, f"{ln}_stats")
                until(dve, b, f"{ln}_stats", k + 1)
                apart(dve)
                for j in range(J):
                    last = dve.bn_aggr(mv[:, n, j, :], stats[:, n, j, :])
                raised(last, f"{ln}_moments")

            def norm(b, n, dst, t, signal):
                ln, k = ln_of(n)
                until(dve, b, f"{ln}_rstd", k + 1)
                for j in range(J):
                    if n == RMS:
                        last = dve.tensor_scalar(dst[:, j, :], t[:, j, :], rstd[:, n, j:j + 1], None, ALU.mult)
                    else:
                        last = dve.tensor_scalar(dst[:, j, :], t[:, j, :], mv[:, n, j, 0:1], rstd[:, n, j:j + 1], ALU.subtract, ALU.mult)
                raised(last, signal)

            def stt(out_, in0, scalar, in1, op0, op1):
                return dve.scalar_tensor_tensor(out=out_, in0=in0, scalar=scalar, in1=in1, op0=op0, op1=op1)

            def mix(b, xT, diff, dst, ready, differ, signal, amounts):
                until(dve, b, ready)
                raised(dve.tensor_tensor(diff[:, :], xT[:, 1:T + 1], xT[:, 0:T], ALU.subtract), differ)
                until(dve, b, differ)
                for t, m in zip(dst, amounts):
                    raised(stt(t[:, :], diff[:, :], v_[m], xT[:, 0:T], ALU.mult, ALU.add), signal)

            def clamp(b, c):
                until(dve, b, "k_ps", c + 1)
                if c >= 2:
                    until(dve, b, "k_first", c - 1)
                raised(dve.tensor_scalar(kk[:, c % 2, :], W[1], K_CLAMP, None, ALU.min), "k_clamped")

            def sums(b, c):
                until(dve, b, "v_ps", c + 1)
                until(dve, b, "k_exp", c + 1)
                raised(dve.tensor_tensor(kvb[:, c % 2, :], kk[:, c % 2, :], W[2], ALU.mult), "kv")
                dc = decay[:, c:c + 1].broadcast_to([P, T])
                raised(dve.tensor_tensor_scan(ksum[:, c % 2, 1:T + 1], dc, kk[:, c % 2, :], 0.0, ALU.mult, ALU.add), "k_sum")
                until(dve, b, "kv", c + 1)
                raised(dve.tensor_tensor_scan(kvsum[:, c % 2, 1:T + 1], dc, kvb[:, c % 2, :], 0.0, ALU.mult, ALU.add), "kv_sum")

            def read(b, c):
                until(dve, b, "kv_sum", c + 1)
                raised(stt(kvb[:, c % 2, :], kvb[:, c % 2, :], first[:, c:c + 1], kvsum[:, c % 2, 0:T], ALU.mult, ALU.add), "wkv")
                until(dve, b, "wk", c + 1)
                raised(dve.reciprocal(wkb[:, c % 2, :], wkb[:, c % 2, :]), "wk_inv")
                until(dve, b, "wkv", c + 1)
                until(dve, b, "r_tanh", c + 1)
                raised(stt(rth[:, c % 2, :], rth[:, c % 2, :], 1.0, kvb[:, c % 2, :], ALU.add, ALU.mult), "gated")

            def first_moments(b):
                dve.wait_ge(sems["x_loaded"], b * 16 + 16)
                moments(b, 0, x0)

            def second_moments(b):
                until(dve, b, "x1_ready")
                moments(b, 1, x1)

            def post_moments(b):
                until(dve, b, "wo_tok_ps")
                raised(dve.tensor_tensor(x2[:, :, :], x1[:, :, :], tok(W[2]), ALU.add), "x2_ready")
                until(dve, b, "x2_ready")
                moments(b, 2, x2)

            def channel_in(b):
                for c in range(C):
                    until(dve, b, "cmk_tanh", c + 1)
                    raised(stt(inner[:, c, :], cth[:, c % 2, :], 1.0, W[1 + c % 2], ALU.add, ALU.mult), "silu")

            def channel_out(b):
                until(dve, b, "cmr_tanh")
                until(dve, b, "cmv_ps")
                raised(stt(cmT[:, :], rth2[:, :], 0.5, W[1], ALU.mult, ALU.add), "cmixT")

            def tree_moments(b):
                until(dve, b, "cmix_tok_ps")
                until(dve, b, "residual")
                raised(stt(y0[:, :, :], tok(W[2]), 0.5, res[:, :, :], ALU.add, ALU.add), "y0")
                until(dve, b, "y0")
                moments(b, 3, y0)

            def tree(b):
                until(dve, b, "gate_tanh")
                raised(dve.tensor_scalar(gate[:, :, 0:NODES], gate[:, :, 0:NODES], 0.5, 0.5, ALU.mult, ALU.add), "gate")
                until(dve, b, "gate")
                src, dst = lpa, lpb
                for level in range(8):
                    n = 2 ** level
                    g = gate[:, :, n - 1:2 * n - 1]
                    pair = dst[:, :, 0:2 * n].rearrange("p j (n s) -> p j n s", s=2)
                    if level == 0:
                        dve.tensor_copy(pair[:, :, :, 1], g)
                        raised(dve.tensor_scalar(pair[:, :, :, 0], g, -1.0, 1.0, ALU.mult, ALU.add), "leaf")
                    else:
                        raised(dve.tensor_tensor(pair[:, :, :, 1], src[:, :, 0:n], g, ALU.mult), "leaf")
                        until(dve, b, "leaf", 2 * level)
                        raised(dve.tensor_tensor(pair[:, :, :, 0], src[:, :, 0:n], pair[:, :, :, 1], ALU.subtract), "leaf")
                    until(dve, b, "leaf", 2 * level + 1)
                    src, dst = dst, src

            def after_tree(b):
                until(dve, b, "ffn_tok_ps")
                raised(dve.tensor_tensor(yb[:, :, :], xb[:, :, :], tok(W[0]), ALU.add), "yb")
                until(dve, b, "yb")
                moments(b, 4, yb)

            def rope_products(b):
                for i in range(4):
                    until(dve, b, "rope_ps", i + 1)
                    raised(dve.tensor_tensor(rope[i], (cos_t if i % 2 == 0 else sin_t)[:, :], S[i % 3], ALU.mult), "rope_mul")

            def row_maxima(b, h):
                for n, j in enumerate(TILE_ORDER):
                    until(dve, b, "rowscore_ps", h * J + (1, 3, 3, 4)[n])
                    raised(dve.tensor_reduce(rmax[:, j, h:h + 1], row_place(j), AX_X, ALU.max), "rowmax")

            def maxima(b):
                until(dve, b, "negmax")
                raised(dve.tensor_copy(mpart[0][:, :], nmax[:, :]), "max_parts")
                until(dve, b, "max_parts", 1)
                raised(dve.tensor_tensor(mrest[:, :], nmax[:, :], mpart[0][:, :], ALU.subtract), "max_rest")
                until(dve, b, "max_rest", 1)
                raised(dve.tensor_copy(mpart[1][:, :], mrest[:, :]), "max_parts")
                until(dve, b, "max_parts", 2)
                raised(dve.tensor_tensor(mpart[2][:, :], mrest[:, :], mpart[1][:, :], ALU.subtract), "max_parts")

            def attended(b, g):
                until(dve, b, "pv_tok_ps", g + 1)
                o = tok(O).rearrange("p j (g r) -> p j g r", r=32)
                raised(dve.reciprocal(pvi[:, :, :], o[:, :, :, DH]), "pv_inv")
                until(dve, b, "pv_inv", g + 1)
                raised(dve.tensor_tensor(att[:, :, :].rearrange("p j (h d) -> p j h d", d=DH)[:, :, 4 * g:4 * g + 4, :], o[:, :, :, 0:DH],
                                         pvi[:, :, :].rearrange("p j (g o) -> p j g o", o=1).broadcast_to([P, J, 4, DH]), ALU.mult), "attn")

            def expert_moments(b):
                until(dve, b, "proj_ps")
                raised(dve.tensor_tensor(yc[:, :, :], kept[:, :, :], tok(S[3]), ALU.add), "yc")
                until(dve, b, "yc")
                moments(b, 6, yc)

            def route(b):
                until(dve, b, "logit_ps")
                ps_lg = S[3][:, 0:J * NE].rearrange("p (j e) -> p j e", j=J)
                raised(dve.tensor_tensor(lg[:, :, :], ps_lg, ebias[:, :].rearrange("p (o e) -> p o e", o=1).broadcast_to([P, J, NE]), ALU.add), "logits")
                until(dve, b, "logits")
                raised(dve.tensor_reduce(lm[:, :], lg[:, :, :], AX_X, ALU.max), "lmax")
                until(dve, b, "lmax")
                raised(dve.tensor_tensor(lsh[:, :, :], lg[:, :, :], wide(lm[:, :], NE), ALU.subtract), "lshift")
                until(dve, b, "lexp")
                raised(dve.tensor_reduce(lsu[:, :], lex[:, :, :], AX_X, ALU.add), "lsum")
                until(dve, b, "lsum")
                raised(dve.reciprocal(lin[:, :], lsu[:, :]), "linv")
                until(dve, b, "linv")
                raised(dve.tensor_tensor(pe_[:, :, :], lex[:, :, :], wide(lin[:, :], NE), ALU.mult), "prob_e")
                until(dve, b, "prob_e")
                ranks = rank[:, :].rearrange("p (o e) -> p o e", o=1).broadcast_to([P, J, NE])
                steps = iter(range(1, 10))

                def pick(ins):
                    raised(ins, "pick")
                    until(dve, b, "pick", next(steps))

                for s, m, eq, key, km, hot in ((pe_, m1, eq1, key1, km1, hot1), (left, m2, eq2, key2, km2, hot2)):
                    pick(dve.tensor_reduce(m[:, :], s[:, :, :], AX_X, ALU.max))
                    pick(dve.tensor_tensor(eq[:, :, :], s[:, :, :], wide(m[:, :], NE), ALU.is_equal))
                    pick(dve.tensor_tensor(key[:, :, :], eq[:, :, :], ranks, ALU.mult))
                    pick(dve.tensor_reduce(km[:, :], key[:, :, :], AX_X, ALU.max))
                    hotted = dve.tensor_tensor(hot[:, :, :], key[:, :, :], wide(km[:, :], NE), ALU.is_equal)
                    if s is pe_:
                        raised(hotted, "hot")
                        until(dve, b, "hot", 1)
                        pick(stt(left[:, :, :], hot1[:, :, :], -2.0, pe_[:, :, :], ALU.mult, ALU.add))
                raised(hotted, "hot")
                until(dve, b, "hot", 2)
                raised(dve.tensor_tensor(hots[:, :, :], hot1[:, :, :], hot2[:, :, :], ALU.add), "hot")
                until(dve, b, "hot", 3)
                raised(dve.tensor_tensor(gts[:, :, :], pe_[:, :, :], hots[:, :, :], ALU.mult), "gates")
                until(dve, b, "gates")
                raised(dve.tensor_copy(gate_part[:, :, 0, :], gts[:, :, :]), "gate_part")
                until(dve, b, "gate_part", 1)
                raised(dve.tensor_tensor(gate_rest[:, :, :], gts[:, :, :], gate_part[:, :, 0, :], ALU.subtract), "gate_part")
                until(dve, b, "gate_part", 2)
                raised(dve.tensor_copy(gate_part[:, :, 1, :], gate_rest[:, :, :]), "gate_part")
                until(dve, b, "gate_part", 3)
                raised(dve.tensor_tensor(gate_part[:, :, 2, :], gate_rest[:, :, :], gate_part[:, :, 1, :], ALU.subtract), "gate_part")

            def expert(b, e):
                until(dve, b, "gb_ps", e + 1)
                raised(dve.tensor_tensor(ug[:, e % 4, :], xdT[:, :], S[3], ALU.mult), "ug")

            def last_moments(b):
                until(dve, b, "moe_tok_ps")
                raised(stt(yd[:, :, :], xd[:, :, :], 2.0, tok(O), ALU.mult, ALU.add), "yd")
                until(dve, b, "yd")
                moments(b, 7, yd)

            def last_norm(b):
                if isinstance(b, int) and b == B - 1:
                    until(dve, b - 1, "stored")
                norm(b, 7, yo, yd, "out_ready")

            turns(dve, {
                "moments0": first_moments, "norm0": lambda b: norm(b, 0, hat, x0, "ln0_hat"),
                "moments1": second_moments, "norm1": lambda b: norm(b, 1, hat, x1, "pre_hat"),
                "mix": lambda b: mix(b, xnT, dif, mixed, "xnT", "mix_diff", "mixed", ("mix_k", "mix_v", "mix_r")),
                **each("clamp", C, clamp), **each("sums", C, sums), **each("read", C, read),
                "moments2": post_moments, "norm2": lambda b: norm(b, 2, hat, x2, "post_hat"),
                "mix2": lambda b: mix(b, xn2T, dif2, mixed2, "xn2T", "mix2_diff", "mixed2", ("cmix_k", "cmix_r")),
                "channel_in": channel_in, "channel_out": channel_out,
                "moments3": tree_moments, "norm3": lambda b: norm(b, 3, xb, y0, "xb_ready"),
                "tree": tree, "moments4": after_tree, "norm4": lambda b: norm(b, 4, xc, yb, "xc_ready"),
                "moments5": lambda b: (until(dve, b, "xc_ready"), moments(b, 5, xc)), "norm5": lambda b: norm(b, 5, xch, xc, "xc_hat"),
                "rope": rope_products, **each("rowmax", NH, row_maxima), "maxima": maxima, **each("back", NQ, attended),
                "moments6": expert_moments, "norm6": lambda b: norm(b, 6, xd, yc, "xd_ready"),
                "route": route, **each("expert", NE, expert),
                "moments7": last_moments, "norm7": last_norm,
                "values_out": lambda b: until(dve, b, "rope_out"),
            })

        @block.tensor
        def _(pe):
            pe.wait_ge(setup["ident"], 6)
            pe.wait_ge(setup["loaded"], ALL_LOADED)
            pe.wait_ge(setup["scaled"], 6)
            pe.wait_ge(setup["rot"], 1)
            pe.wait_ge(setup["brow_parts"], 6)
            for n, (src, rows, _) in enumerate(TURNS):
                if n >= 8:
                    pe.wait_ge(setup["turned"], n - 7)
                pe.transpose(bank[n % 8][:, 0:rows], src, ident[0:rows, 0:rows]).then_inc(setup["turned_ps"], 1)
            pe.wait_ge(setup["turned"], len(TURNS))
            pe.matmul(bank[0][:, 0:NODES], tq, routersT[:, 0:NODES], start=True, stop=True).then_inc(setup["fused_ps"], 1)
            for k in range(2):
                last = pe.matmul(bank[1][:, k * P:(k + 1) * P], leavesT[:, k * P:(k + 1) * P], woutT, start=True, stop=True)
            last.then_inc(setup["fused_ps"], 1)
            pe.wait_ge(setup["fused"], 2)

            def turn(bk, t, signal):
                for j in range(J):
                    last = pe.transpose(bk[:, j * P:(j + 1) * P], t[:, j, :], ident[:, :])
                raised(last, signal)

            def mm(out_, w, x, start=True, stop=True, **kw):
                return pe.matmul(out_, w, x, start=start, stop=stop, **kw)

            def tiles(t):
                return t[:, :].rearrange("p (j h) -> p j h", j=J)

            def turn_when(ready, bk, t, signal):
                return lambda b: (until(pe, b, ready), turn(bk, t, signal))

            def project(b, c):
                cs = slice(c * P, (c + 1) * P)
                for i, (w, bk, done, freed) in enumerate(((wk, W[1], "k_ps", "k_clamped"), (wv, W[2], "v_ps", "kv"), (wr, W[0], "r_ps", "r_tanh"))):
                    until(pe, b, "mixed", i + 1) if c == 0 else until(pe, b, freed, c)
                    raised(mm(bk, w[:, cs], mixed[i][:, :]), done)

            def read_out(b):
                until(pe, b, "k_clamped")
                for c in range(C):
                    until(pe, b, "rwkv", c + 1)
                    last = mm(W[1], wo[:, c, :], inner[:, c, :], c == 0, c == C - 1)
                raised(last, "wo_ps")
                until(pe, b, "woT")
                turn(W[2], tiles(woT), "wo_tok_ps")

            def channel_in(b):
                until(pe, b, "mixed2", 1)
                for c in range(C):
                    if c >= 2:
                        until(pe, b, "silu", c - 1)
                    raised(mm(W[1 + c % 2], cwk[:, c * P:(c + 1) * P], mixed2[0][:, :]), "cmk_ps")
                until(pe, b, "mixed2", 2)
                raised(mm(W[0], cwr[:, :], mixed2[1][:, :]), "cmr_ps")

            def channel_out(b):
                for c in range(C):
                    until(pe, b, "silu", max(c + 1, 3))
                    last = mm(W[1], cwv[:, c, :], inner[:, c, :], c == 0, c == C - 1)
                raised(last, "cmv_ps")
                until(pe, b, "cmixT")
                turn(W[2], tiles(cmT), "cmix_tok_ps")

            def gates(b):
                until(pe, b, "xbT")
                for k in range(2):
                    for j in range(2 * k, 2 * k + 2):
                        last = mm(W[1 + k][:, (j % 2) * LEAVES:(j % 2) * LEAVES + NODES], xbT[:, j * P:(j + 1) * P], w_gate[:, 0:NODES])
                    raised(last, "gate_ps")

            def leaves_out(b):
                until(pe, b, "leaf")
                for k in range(2):
                    turn(W[k], lpa[:, :, k * P:(k + 1) * P], "leafT_ps")
                for k in range(2):
                    until(pe, b, "leafT", k + 1)
                    last = mm(W[2], w_leaf[:, k, :], lpT[:, k, :], k == 0, k == 1)
                raised(last, "ffn_ps")
                until(pe, b, "ffnT")
                turn(W[0], tiles(ffnT), "ffn_tok_ps")

            def rope_products(b):
                until(pe, b, "xcT")
                for i in range(4):
                    if i == 3:
                        until(pe, b, "rope_mul", 1)
                    raised(mm(S[i % 3], w_rope[:, i, :, :].rearrange("p d h -> p (d h)"), xcT[:, :]), "rope_ps")
                for j in range(J):
                    last = mm(O[:, j * P:(j + 1) * P], xcT[:, j * P:(j + 1) * P], av[:, :])
                raised(last, "v_tok_ps")

            def row_scores(b, h):
                if h == 0:
                    until(pe, b, "rope_mul")
                    until(pe, b, "heads_in")
                for n, j in enumerate(TILE_ORDER):
                    if h and n != 1:
                        until(pe, b, "rowmax", (h - 1) * J + {0: 1, 2: 3, 3: 4}[n])
                    elif h:
                        until(pe, b, "rowmax", (h - 1) * J + 3)
                    q, to = qh[0:KROWS, h, j * P:(j + 1) * P], row_place(j)
                    mm(to, q, kh[0:KROWS, h, 0:(j + 1) * P], True, False, skip_group_check=True)
                    raised(mm(to[:, j * P:(j + 1) * P], identb[:, :], maskb[:, :], False, True, skip_group_check=True), "rowscore_ps")

            def maxima(b):
                until(pe, b, "rowmax")
                for j in range(J):
                    last = pe.transpose(S[0][0:NH, j * P:(j + 1) * P], rmax[:, j, :], ident[:, :])
                raised(last, "maxT_ps")

            def score(b, n):
                g, u = n // 5, n % 5
                if n == 0:
                    until(pe, b, "negmax")
                    until(pe, b, "max_in")
                elif n >= 2:
                    until(pe, b, "prob", n - 1)
                for s in range(2):
                    bk = SD[n % 2][:, s * T:(s + 1) * T]
                    h = 4 * g + 2 * (u % 2) + s
                    for head, i, col in ([(h, 0, 0)], [(h, 1, 0), (h, 3, 3 * P)], [(4 * g + 2 * s, 2, 0), (4 * g + 2 * s + 1, 2, 2 * P)])[u // 2]:
                        mm(bk[:, col:col + T - i * P], kh[:, head, i * P:(i + 1) * P], qh[:, head, i * P:T], True, False, skip_group_check=True)
                        last = mm(bk[:, col:col + P], identb[:, :], maskTb[:, :], False, True, skip_group_check=True)
                raised(last, "score_ps")

            def weigh(b, g):
                until(pe, b, "vaug") if g == 0 else until(pe, b, "attn", g)
                for i, pairs, unit in ((0, 2, lambda q: (q, 0)), (1, 4, lambda q: (4 + q, 0)), (3, 4, lambda q: (4 + q, 3 * P)),
                                       (2, 5, lambda q: (8 + q // 2, (q % 2) * 2 * P))):
                    if i != 3:
                        until(pe, b, "prob", 5 * g + pairs)
                    for q in range(4):
                        u, col = unit(q)
                        last = mm(O[32 * q:32 * q + 32, i * P:T], vaug[:, i, 4 * g + q, :], prob[:, u, col:col + T - i * P],
                                  i == 0, i == 2, tile_position=(0, 32 * q), skip_group_check=True)
                    if i != 1:
                        raised(last, "pv_ps")

            def attn_project(b):
                until(pe, b, "attn")
                until(pe, b, "prob")
                turn(S[3], att, "attnT_ps")
                until(pe, b, "attnT")
                for j in range(J):
                    last = mm(S[3][:, j * P:(j + 1) * P], attT[:, j * P:(j + 1) * P], ao[:, :])
                raised(last, "proj_ps")

            def turn_experts(b):
                until(pe, b, "xd_ready")
                turn(S[3], xd, "xdT_ps")
                until(pe, b, "xdT")
                for j in range(J):
                    last = mm(S[3][:, j * NE:(j + 1) * NE], xdT[:, j * P:(j + 1) * P], centT[:, :])
                raised(last, "logit_ps")

            def turn_gates(b):
                until(pe, b, "gate_part")
                for j in range(J):
                    last = mm(S[3][0:PARTS * NE, j * P:(j + 1) * P], gate_part[:, j, :, :].rearrange("p i e -> p (i e)"), identb[:, :])
                raised(last, "gT_ps")

            def start_experts(b):
                mm(O, wshT[:, :], xdT[:, :], True, False, skip_group_check=True)
                until(pe, b, "gT")
                for i in range(PARTS):
                    mm(O, brow_part[:, i, :], gT[:, :], False, False, skip_group_check=True)

            def expert(b, e):
                if e:
                    until(pe, b, "ug", e)
                raised(mm(S[3], owner[:, e:e + 1].broadcast_to([PARTS * NE, P]), gT[:, :]), "gb_ps")
                if e:
                    mm(O, wexpT[:, e - 1, :], ug[:, (e - 1) % 4, :], False, False, skip_group_check=True)

            def experts_out(b):
                until(pe, b, "ug")
                raised(mm(O, wexpT[:, NE - 1, :], ug[:, (NE - 1) % 4, :], False, True, skip_group_check=True), "moe_ps")
                until(pe, b, "moeT")
                turn(O, tiles(moT), "moe_tok_ps")

            turns(pe, {
                "turn_pre": turn_when("pre_hat", W[0], hat, "xnT_ps"), **each("project", C, project), "read_out": read_out,
                "turn_post": turn_when("post_hat", W[0], hat, "xn2T_ps"), "channel_in": channel_in, "channel_out": channel_out,
                "turn_tree": turn_when("xb_ready", W[0], xb, "xbT_ps"), "gates": gates, "leaves": leaves_out,
                "turn_in": turn_when("xc_hat", S[0], xch, "xcT_ps"), "rope": rope_products, **each("rowmax", NH, row_scores),
                "maxima": maxima, **each("score", 5 * NQ, score), **each("weigh", NQ, weigh),
                **each("back", NQ, lambda b, g: (until(pe, b, "pvT", g + 1), turn(O, tiles(pvT), "pv_tok_ps"))),
                "project": attn_project, "turn_experts": turn_experts, "turn_gates": turn_gates,
                "start_experts": start_experts, **each("expert", NE, expert), "experts_out": experts_out,
                "o_free": lambda b: until(pe, b, "yd"), "values_out": lambda b: until(pe, b, "vaug"),
            })


_UNUSED = ["L0_ffn_leaf_keys"]
_ROPE_BASE = 1000000.0


def _rope_tables():
    import numpy as np
    half = DH // 2
    theta = (1.0 / np.power(np.float32(_ROPE_BASE), (2 * np.arange(half) / DH).astype(np.float32))).astype(np.float32)
    angles = (theta[:, None] * np.arange(T, dtype=np.float32)[None, :]).astype(np.float32)
    rows = np.repeat(np.tile(angles, (2, 1)), NH, axis=0)
    return np.cos(rows).astype(np.float32), np.sin(rows).astype(np.float32)


def kernel(**inputs):
    import numpy as _np
    import concourse.bacc as _bacc
    from concourse.bass_utils import run_bass_kernel_spmd as _run

    nc = _bacc.Bacc("TRN2", target_bir_lowering=False, num_devices=1)
    arrays, args = {}, {}
    given = {n: _np.ascontiguousarray(v) for n, v in inputs.items() if n not in _UNUSED}
    given["rope_cos"], given["rope_sin"] = _rope_tables()
    for name, v in given.items():
        arrays[f"in_{name}_dram"] = v
        args[name] = nc.dram_tensor(f"in_{name}_dram", v.shape, mybir.dt.from_np(v.dtype), kind="ExternalInput").ap()
    out = nc.dram_tensor("out_0_dram", (B, T, P), F32, kind="ExternalOutput").ap()
    build(nc, args, out)
    r = _run(nc, [arrays], core_ids=[0])
    return r.results[0]["out_0_dram"]
```

```python
from contextlib import ExitStack

import concourse.bass as bass
from concourse import mybir

ALU = mybir.AluOpType
ACT = mybir.ActivationFunctionType
F32 = mybir.dt.float32
BF16 = mybir.dt.bfloat16
AX_X = mybir.AxisListType.X

P = 128
B = 16
T = 512
J = T // P
HU = 512
C = HU // P
NODES = 255
LEAVES = 256
NH = 16
DH = 8
RMS = 5
NQ = NH // 4
PARTS = 3
KROWS = PARTS * PARTS * DH
KALL = KROWS + PARTS
NE = 16
LN_EPS, RMS_EPS, K_EPS = 1e-5, 1e-6, 1e-8
K_CLAMP = 60.0
MASKED = -1e30

PER_BATCH = dict(
    x_loaded=16, ln_stats=4, ln_moments=4, ln_minus=4, ln_var=4, ln_rstd=4, ln_shift=4, ln2_stats=2, ln2_moments=2, ln2_minus=1, ln2_var=3, ln2_rstd=2, ln2_shift=1,
    ln3_stats=2, ln3_moments=2, ln3_minus=2, ln3_var=2, ln3_rstd=2, ln3_shift=2, xc_kept=1, ln0_hat=1, ln0_gain=1, x1_ready=1, pre_hat=1,
    xnT_ps=1, xnT=1, mix_diff=1, mixed=3, k_ps=4, v_ps=4, r_ps=4, k_exp=4, r_tanh=4, k_clamped=4, kv=4,
    k_sum=4, kv_sum=4, k_first=4, wk=4, wk_inv=4, wkv=4, r_one=4, gated=4, rwkv=4, wo_ps=1, woT=1, wo_tok_ps=1, x2_ready=1,
    residual=1, post_hat=1, xn2T_ps=1, xn2T=1, mix2_diff=1, mixed2=2, cmk_ps=4, cmk_tanh=4, silu=4, cmr_ps=1, cmr_tanh=1,
    cmv_ps=1, cmixT=1, cmix_tok_ps=1, y0=1, xb_ready=1,
    xbT_ps=1, xbT=1, gate_ps=2, gate_tanh=2, gate=1, leaf=15, leafT_ps=2, leafT=2, ffn_ps=1, ffnT=1, ffn_tok_ps=1,
    yb=1, xc_ready=1,
    xc_hat=1, xcT_ps=1, xcT=1, rope_ps=4, v_tok_ps=1, v_out=1, vaug=1, rope_mul=4, rope_out=2, part1=2, rest1=2, part2=2, part3=2,
    heads_in=16 * 2 * PARTS * PARTS, rowscore_ps=64, rowmax=64, maxT_ps=1, negmax=1, max_rest=1, max_parts=3, max_in=48,
    score_ps=20, prob=20, pv_ps=12, pvT=4, pv_tok_ps=4, pv_inv=4, attn=4,
    attnT_ps=1, attnT=1, proj_ps=1, yc=1, xd_ready=1,
    xdT_ps=1, xdT=1, logit_ps=1, logits=1, lmax=1, lshift=1, lexp=1, lsum=1, linv=1, prob_e=1, pick=9, hot=3, gates=1,
    gate_part=4, gT_ps=1, gT=1, gb_ps=16, ug=8, spread_out=8, ug_side=8, moe_ps=1, moeT=1, moe_tok_ps=1, yd=1, out_ready=1, stored=16,
)


def build(nc: bass.Bass, a, out):
    with ExitStack() as ctx:
        def sb(name, shape, dt=F32):
            return ctx.enter_context(nc.sbuf_tensor(name, shape, dt))

        sems = {n: ctx.enter_context(nc.semaphore(f"s_{n}")) for n in PER_BATCH}
        setup = {n: ctx.enter_context(nc.semaphore(f"w_{n}")) for n in
                 ("loaded", "brow_parts", "ident0", "ident", "consts", "scaled", "decay1", "decay", "turned_ps", "turned", "fused_ps", "fused", "rot", "ones")}

        passed = {e: ctx.enter_context(nc.semaphore(f"s_passed_{e.name}")) for e in (nc.sync.engine, nc.vector.engine, nc.gpsimd.engine)}

        def raised(ins, name, by=1):
            ins.then_inc(sems[name], by)

        def until(eng, b, name, n=None):
            per = PER_BATCH[name]
            eng.wait_ge(sems[name], b * per + (per if n is None else n))

        def ln_of(n):
            return ("ln", n) if n < 4 else ("ln2", n - 4) if n < 6 else ("ln3", n - 6)

        def apart(eng):
            eng.sem_inc(passed[eng.engine], 1)

        wk, wv, wr, cwk = (sb(n, [P, HU]) for n in ("wk", "wv", "wr", "cwk"))
        wo, cwv = (sb(n, [P, C, P]) for n in ("wo", "cwv"))
        cwr = sb("cwr", [P, P])
        vec_names = ["pre_g", "pre_b", "post_g", "post_b", "mix_k", "mix_v", "mix_r", "cmix_k", "cmix_r", "norm_scale", "wout_b"]
        vec = sb("vec", [P, len(vec_names)])
        v_ = {n: vec[:, i:i + 1] for i, n in enumerate(vec_names)}
        tdec, tfirst, dec_e, decay, first = (sb(n, [P, C]) for n in ("tdec", "tfirst", "dec_e", "decay", "first"))
        g0, b0 = sb("g0", [P, P]), sb("b0", [P, P])
        w_gate, w_leaf = sb("w_gate", [P, LEAVES]), sb("w_leaf", [P, 2, P])
        aq, ak, av, ao = (sb(n, [P, P]) for n in ("aq", "ak", "av", "ao"))
        w_rope = sb("w_rope", [P, 4, DH, NH])
        cos_t, sin_t = sb("cos_t", [P, T]), sb("sin_t", [P, T])
        cent, centT, ebias = sb("cent", [NE, P]), sb("centT", [P, NE]), sb("ebias", [P, NE])
        wexpT = sb("wexpT", [P, NE, P])
        prob = sb("prob", [P, 10, T])
        came = prob[:, :, :].rearrange("p u (k h) -> p (u k) h", h=P)
        wexp, routers, leaves, wsh = came[:, 0:16, :], came[:, 16:18, :], came[:, 18:20, :], came[:, 20:22, :]
        tq, wout, wshs, woutT = (came[:, k, :] for k in (22, 23, 24, 25))
        routersT, leavesT = prob[:, 7, 0:LEAVES], prob[:, 7, LEAVES:2 * LEAVES]
        brow, brow_rest = came[0:PARTS * NE, 32, :], came[0:PARTS * NE, 33, :]
        brow_part = sb("brow_part", [PARTS * NE, PARTS, P], BF16)
        owner = sb("owner", [PARTS * NE, NE], BF16)
        wshT = sb("wshT", [P, P])
        bsh, bshs = sb("bsh", [P, 2]), sb("bshs", [P, 1])
        ident, identb = sb("ident", [P, P]), sb("identb", [P, P], BF16)
        maskb, maskTb = sb("maskb", [P, P], BF16), sb("maskTb", [P, P], BF16)
        rank = sb("rank", [P, NE])
        eps_ln, eps_rms = sb("eps_ln", [P, J]), sb("eps_rms", [P, J])
        exponent, minus_one = sb("exponent", [P, J]), sb("minus_one", [P, J])
        keps = sb("keps", [P, 1])

        x0, x1, hat, x2, res = (sb(n, [P, J, P]) for n in ("x0", "x1", "hat", "x2", "res"))
        stats, mv, rstd = sb("stats", [P, 8, J, 6]), sb("mv", [P, 8, J, 2]), sb("rstd", [P, 8, J])
        var, minus, shift = sb("var", [P, 8, J]), sb("minus", [P, 8, J]), sb("shift", [P, 8, J])
        xnT, xn2T = sb("xnT", [P, T + 1]), sb("xn2T", [P, T + 1])
        dif = dif2 = sb("dif", [P, T])
        mixed = [sb(f"mixed{i}", [P, T]) for i in range(3)]
        mixed2 = mixed[0:2]
        kk, kvb, wkb, rth = (sb(n, [P, 2, T]) for n in ("kk", "kvb", "wkb", "rth"))
        inner = sb("inner", [P, C, T])
        ksum, kvsum = sb("ksum", [P, 2, T + 1]), sb("kvsum", [P, 2, T + 1])
        woT = sb("woT", [P, T])
        cth = sb("cth", [P, 2, T])
        rth2, cmT = sb("rth2", [P, T]), woT
        xb, xc = (sb(n, [P, J, P]) for n in ("xb", "xc"))
        y0, yb = x1, x2
        xbT = sb("xbT", [P, T])
        gate, lpa, lpb = (t[:, :, :].rearrange("p u (j n) -> p (u j) n", j=2) for t in (kk, kvb, rth))
        lpT = inner[:, 0:2, :]
        ffnT = woT
        kept = sb("kept", [P, J, P])
        xd, yo, att = (sb(n, [P, J, P]) for n in ("xd", "yo", "att"))
        yc, yd = sb("yc", [P, J, P]), att
        xch = values = sb("values", [P, J, P])
        xcT = sb("xcT", [P, T])
        rope = [sb(f"rope{i}", [P, T]) for i in range(4)]
        qk = [rope[2 * i][:, :] for i in range(2)]
        rest = [rope[2 * i + 1][:, :] for i in range(2)]
        part = [[sb(f"part{i}{j}", [P, T], BF16) for j in range(PARTS)] for i in range(2)]
        qh, kh = sb("qh", [KALL, NH, T], BF16), sb("kh", [KALL, NH, T], BF16)
        vaug = sb("vaug", [P, J, NH, 32])
        rmax = sb("rmax", [P, J, NH])
        nmax, mrest = sb("nmax", [NH, T]), xcT[0:NH, :]
        mpart = [sb(f"mpart{i}", [NH, T], BF16) for i in range(PARTS)]
        pvT = sb("pvT", [P, T])
        pvi = sb("pvi", [P, J, 4])
        attT = pvT
        xdT = sb("xdT", [P, T])
        lg, lsh, lex, pe_, gts = (sb(n, [P, J, NE]) for n in ("lg", "lsh", "lex", "pe_", "gts"))
        lm, lsu, lin = (sb(n, [P, J]) for n in ("lm", "lsu", "lin"))
        eq1, key1, hot1, left, eq2, key2, hot2, hots = (sb(n, [P, J, NE]) for n in
            ("eq1", "key1", "hot1", "left", "eq2", "key2", "hot2", "hots"))
        m1, km1, m2, km2 = (sb(n, [P, J]) for n in ("m1", "km1", "m2", "km2"))
        gate_part, gate_rest = sb("gate_part", [P, J, PARTS, NE], BF16), sb("gate_rest", [P, J, NE])
        gT = sb("gT", [PARTS * NE, T], BF16)
        ug = prob[:, 0:4, :]
        spread = [t[:, :] for t in rope[0:2]]
        moT = pvT

        ps = [ctx.enter_context(nc.psum_tensor(f"bank{i}", [P, 1024], F32)) for i in range(4)]
        bank = [ps[i // 2][:, (i % 2) * 512:(i % 2) * 512 + 512] for i in range(8)]
        S, O, W = bank[0:4], bank[4], bank[5:8]
        SD = [ps[0], ps[1]]

        def tok(bk):
            return bk.rearrange("p (j h) -> p j h", j=J)

        def wide(t2, n):
            return t2.rearrange("p (j o) -> p j o", o=1).broadcast_to([P, J, n])

        TILE_ORDER = (3, 0, 2, 1)
        ROPE_BANK = (1, 2, 0, 1)

        def row_place(j):
            bk, col = {3: (S[0], 0), 0: (S[2], 0), 2: (S[2], P), 1: (S[1], 0)}[j]
            return bk[:, col:col + (j + 1) * P]

        block = ctx.enter_context(nc.Block())

        LOADS = [
            (wk[:, :], a["L0_attn_tm_Wk"]), (wv[:, :], a["L0_attn_tm_Wv"]), (wr[:, :], a["L0_attn_tm_Wr"]),
            (cwk[:, :], a["L0_attn_cm_Wk"]), (cwr[:, :], a["L0_attn_cm_Wr"]),
            (wo[:, :, :], a["L0_attn_tm_Wo"].rearrange("(c p) h -> p c h", p=P)),
            (cwv[:, :, :], a["L0_attn_cm_Wv"].rearrange("(c p) h -> p c h", p=P)),
            (tdec[:, :], a["L0_attn_tm_decay"].rearrange("(c p) -> p c", p=P)),
            (tfirst[:, :], a["L0_attn_tm_first"].rearrange("(c p) -> p c", p=P)),
            (g0[:, :], a["L0_attn_ln0_g"].rearrange("(o h) -> o h", o=1).broadcast_to([P, P])),
            (b0[:, :], a["L0_attn_ln0_b"].rearrange("(o h) -> o h", o=1).broadcast_to([P, P])),
            (tq[:, :], a["L0_ffn_Wq"]), (wout[:, :], a["L0_ffn_Wout_w"]),
            (routers[:, 0, :], a["L0_ffn_routers"][0:P, :]), (routers[0:NODES - P, 1, :], a["L0_ffn_routers"][P:NODES, :]),
            (leaves[:, :, :], a["L0_ffn_leaf_values"].rearrange("(k p) h -> p k h", p=P)),
            (aq[:, :], a["L1_attn_Wq"]), (ak[:, :], a["L1_attn_Wk"]), (av[:, :], a["L1_attn_Wv"]), (ao[:, :], a["L1_attn_Wo"]),
            (cos_t[:, :], a["rope_cos"]), (sin_t[:, :], a["rope_sin"]),
            (cent[:, :], a["L1_ffn_centroids"]),
            (ebias[:, :], a["L1_ffn_expert_biases"].rearrange("(o e) -> o e", o=1).broadcast_to([P, NE])),
            (wexp[:, :, :], a["L1_ffn_Wr"].rearrange("e o d -> o e d")), *((brow[i * NE:(i + 1) * NE], a["L1_ffn_br"]) for i in range(PARTS)),
            (wsh[:, :, :], a["L1_ffn_Ws"].rearrange("n o d -> o n d")), (bsh[:, :], a["L1_ffn_bs"].rearrange("n o -> o n")),
        ]
        for n, src in (("pre_g", "L0_attn_pre_g"), ("pre_b", "L0_attn_pre_b"), ("post_g", "L0_attn_post_g"), ("post_b", "L0_attn_post_b"),
                       ("mix_k", "L0_attn_tm_mix_k"), ("mix_v", "L0_attn_tm_mix_v"), ("mix_r", "L0_attn_tm_mix_r"),
                       ("cmix_k", "L0_attn_cm_mix_k"), ("cmix_r", "L0_attn_cm_mix_r"), ("norm_scale", "L1_attn_norm_scale"),
                       ("wout_b", "L0_ffn_Wout_b")):
            LOADS.append((v_[n], a[src].rearrange("(p o) -> p o", o=1)))
        ALL_LOADED = 16 * len(LOADS)

        TURNS = [(routers[:, 0, :], P, routersT[:, 0:P]), (routers[0:NODES - P, 1, :], NODES - P, routersT[:, P:NODES]),
                 (leaves[:, 0, :], P, leavesT[:, 0:P]), (leaves[:, 1, :], P, leavesT[:, P:2 * P]),
                 (wout[:, :], P, woutT[:, :]), (cent[:, :], NE, centT[:, :]), (wshs[:, :], P, wshT[:, :])]
        TURNS += [(wexp[:, e, :], P, wexpT[:, e, :]) for e in range(NE)]

        ORDER = """
            t:moments0 e:score0 a:tree a:level0 e:score1 a:level1 a:level2 a:level3 a:level4 a:level5 a:level6
            e:score2 e:score3 e:score4 a:level7 a:leaves t:norm0 a:leaf_sum e:score5 e:score6 a:leaf_turn
            e:weigh0 e:sum_out0 e:score7 a:moments4 a:norm4 e:back0 e:score8 e:score9 a:moments5 a:norm5
            e:score10 e:score11 t:moments1 e:weigh1 a:turn_in t:norm1 e:score12 e:score13 a:rope e:sum_out1
            a:w_free t:turn_pre t:mix e:score14 e:back1 t:project0 t:clamp0 a:parts t:sums0 e:score15 e:score16
            e:weigh2 e:score17 e:sum_out2 e:score18 t:read0 t:clamp1 t:project1 e:back2 t:sums1 e:score19
            t:clamp2 t:project2 t:read1 t:sums2 e:weigh3 e:sum_out3 e:back3 t:clamp3 t:project3 e:project
            e:attn_out t:read2 e:moments6 t:sums3 a:rowmax0 e:norm6 e:turn_experts t:read3 e:centroids e:route
            a:rowmax1 e:route_probs t:read_out e:largest0 e:largest1 e:largest2 e:largest3 e:largest4 e:others
            e:largest5 e:largest6 t:read_turn e:largest7 e:largest8 e:largest9 e:route_gates e:gate_parts
            t:moments2 e:turn_gates a:rowmax2 e:start_experts t:norm2 e:expert0 a:rowmax3 e:expert1 a:rowmax4
            t:turn_post e:expert2 a:rowmax5 e:expert3 e:expert4 t:mix2 a:rowmax6 e:expert5 t:channel_in0
            e:expert6 t:channel_in1 a:rowmax7 e:expert7 t:channel_in4 e:expert8 a:rowmax8 e:expert9 a:rowmax9
            e:expert10 a:rowmax10 t:channel_in2 e:expert11 a:rowmax11 e:expert12 t:channel_in3 a:rowmax12
            t:channel_out a:rowmax13 e:expert13 e:expert14 t:channel_turn t:moments3 e:expert15 a:rowmax14
            e:experts_out a:rowmax15 t:norm3 e:experts_turn e:moments7 a:maxima t:turn_tree a:place_values
            t:gates e:norm7 e:o_free a:keep
        """.split()

        def run(steps, b_t, b_a, b_e):
            for name in ORDER:
                b = {"t": b_t, "a": b_a, "e": b_e}[name[0]]
                if b is not None and name[2:] in steps:
                    steps[name[2:]](b)

        def turns(eng, steps):
            run(steps, 0, None, None)
            run(steps, 1, 0, None)
            with eng.Fori(2, B) as b:
                run(steps, b, b - 1, b - 2)
            run(steps, None, B - 1, B - 2)
            run(steps, None, None, B - 1)

        def each(name, n, f):
            return {f"{name}{k}": (lambda b, k=k: f(b, k)) for k in range(n)}

        @block.sync
        def _(sp):
            sp.dma_start(x0[:, :, :], a["L0_attn_x"][0].rearrange("(j p) h -> p j h", p=P)).then_inc(sems["x_loaded"], 16)
            for dst, src in LOADS:
                sp.dma_start(dst, src, allow_slow_non_contiguous=True).then_inc(setup["loaded"], 16)

            def load_next(b):
                until(sp, b, "residual")
                apart(sp)
                src = a["L0_attn_x"][bass.ds(b + 1, 1)].rearrange("o (j p) h -> p (o j) h", p=P)
                sp.dma_start(x0[:, :, :], src).then_inc(sems["x_loaded"], 16)

            def spread_heads(b, used=True):
                if used:
                    until(sp, b - 1, "score_ps")
                for t, dst in enumerate((qh, kh)):
                    for m in range(PARTS):
                        until(sp, b, f"part{m + 1}", t + 1)
                        for o in range(PARTS):
                            r = (m * PARTS + o if t == 0 else o * PARTS + m) * DH
                            sp.dma_start(dst[r:r + DH, :, :], part[t][m][:, :]).then_inc(sems["heads_in"], 16)

            def spread_maxima(b):
                for i in range(PARTS):
                    until(sp, b, "max_parts", i + 1)
                    sp.dma_start(qh[KROWS + i:KROWS + i + 1, :, :], mpart[i][:, :]).then_inc(sems["max_in"], 16)

            def store(b):
                until(sp, b, "out_ready")
                apart(sp)
                dst = out[bass.ds(b, 1)].rearrange("o (j p) h -> p (o j) h", p=P)
                sp.dma_start(dst, yo[:, :, :]).then_inc(sems["stored"], 16)
                apart(sp)
                until(sp, b, "stored")
                apart(sp)

            load_next(0)
            spread_heads(0, used=False)
            load_next(1)
            spread_maxima(0)
            with sp.Fori(2, B - 1) as b:
                spread_heads(b - 1)
                load_next(b)
                spread_maxima(b - 1)
                store(b - 2)
            for b in (B - 1, B):
                spread_heads(b - 1)
                spread_maxima(b - 1)
                store(b - 2)
            store(B - 1)

        @block.gpsimd
        def _(pool):
            zeroed = (ident[:, :], identb[:, :], maskb[:, :], maskTb[:, :], vaug[:, :, :, :], ksum[:, :, 0:1], kvsum[:, :, 0:1],
                      xnT[:, 0:1], xn2T[:, 0:1])
            filled = ((exponent[:, :], -0.5), (minus_one[:, :], -1.0), (eps_ln[:, :], LN_EPS), (eps_rms[:, :], RMS_EPS), (keps[:, :], K_EPS), (kh[:, :, :], 1.0))
            for t, value in (*((z, 0.0) for z in zeroed), *filled):
                pool.memset(t, value).then_inc(setup["ident0"], 1)
            pool.wait_ge(setup["ident0"], len(zeroed) + len(filled))
            for t, op, fill, step in ((ident, ALU.not_equal, 1.0, -1), (identb, ALU.not_equal, 1.0, -1),
                                      (maskb, ALU.is_ge, MASKED, -1),
                                      (maskTb, ALU.is_ge, MASKED, 1)):
                pool.affine_select(out=t[:, :], in_=t[:, :], compare_op=op, fill=fill, base=0,
                                   pattern=[[step, P]], channel_multiplier=-step).then_inc(setup["ident"], 1)
            pool.iota(rank[:, :], pattern=[[-1, NE]], base=NE, channel_multiplier=0,
                      allow_small_or_imprecise_dtypes=True).then_inc(setup["ident"], 1)
            pool.memset(vaug[:, :, :, DH:DH + 1], 1.0).then_inc(setup["ident"], 1)
            pool.wait_ge(setup["ident"], 6)

            def inverse_root(b, n):
                ln, k = ln_of(n)
                until(pool, b, f"{ln}_moments", k + 1)
                raised(pool.tensor_tensor(var[:, n, :], mv[:, n, :, 1], eps_ln[:, :], ALU.add), f"{ln}_var")
                until(pool, b, f"{ln}_var", k + 1)
                raised(pool.tensor_tensor(rstd[:, n, :], var[:, n, :], exponent[:, :], ALU.pow), f"{ln}_rstd")
                raised(pool.tensor_tensor(minus[:, n, :], mv[:, n, :, 0], minus_one[:, :], ALU.mult), f"{ln}_minus")
                until(pool, b, f"{ln}_rstd", k + 1)
                until(pool, b, f"{ln}_minus", k + 1)
                raised(pool.tensor_tensor(shift[:, n, :], minus[:, n, :], rstd[:, n, :], ALU.mult), f"{ln}_shift")

            def inverse_rms(b):
                until(pool, b, "ln2_moments", 2)
                pool.tensor_tensor(var[:, RMS, :], mv[:, RMS, :, 1], eps_rms[:, :], ALU.add)
                raised(pool.tensor_tensor(rstd[:, RMS, :], mv[:, RMS, :, 0], mv[:, RMS, :, 0], ALU.mult), "ln2_var")
                until(pool, b, "ln2_var", 2)
                raised(pool.tensor_tensor(mv[:, RMS, :, 1], var[:, RMS, :], rstd[:, RMS, :], ALU.add), "ln2_var")
                until(pool, b, "ln2_var", 3)
                raised(pool.tensor_tensor(rstd[:, RMS, :], mv[:, RMS, :, 1], exponent[:, :], ALU.pow), "ln2_rstd")

            def over_tiles(t):
                return t.rearrange("p (o h) -> p o h", o=1).broadcast_to([P, J, P])

            def first_gain(b):
                until(pool, b, "ln0_hat")
                raised(pool.tensor_tensor(hat[:, :, :], hat[:, :, :], over_tiles(g0[:, :]), ALU.mult), "ln0_gain")
                until(pool, b, "ln0_gain")
                raised(pool.tensor_tensor(x1[:, :, :], hat[:, :, :], over_tiles(b0[:, :]), ALU.add), "x1_ready")

            def rope_sum(b):
                for t in range(2):
                    until(pool, b, "rope_mul", 2 * t + 2)
                    raised(pool.tensor_tensor(qk[t], rope[2 * t][:, :], rope[2 * t + 1][:, :], ALU.add), "rope_out")

            def parts(b):
                for t in range(2):
                    until(pool, b, "part1", t + 1)
                    raised(pool.tensor_tensor(rest[t], qk[t], part[t][0][:, :], ALU.subtract), "rest1")
                for t in range(2):
                    until(pool, b, "part2", t + 1)
                    raised(pool.tensor_tensor(part[t][2][:, :], rest[t], part[t][1][:, :], ALU.subtract), "part3")

            def read(b, c):
                until(pool, b, "k_first", c + 1)
                until(pool, b, "k_sum", c + 1)
                raised(pool.tensor_tensor(wkb[:, c % 2, :], wkb[:, c % 2, :], ksum[:, c % 2, 0:T], ALU.add), "wk")
                until(pool, b, "r_tanh", c + 1)
                apart(pool)
                raised(pool.tensor_scalar(rth[:, c % 2, :], rth[:, c % 2, :], 1.0, None, ALU.add), "r_one")
                until(pool, b, "r_one", c + 1)
                until(pool, b, "wkv", c + 1)
                raised(pool.tensor_tensor(rth[:, c % 2, :], rth[:, c % 2, :], kvb[:, c % 2, :], ALU.mult), "gated")
                until(pool, b, "gated", c + 1)
                until(pool, b, "wk_inv", c + 1)
                raised(pool.tensor_tensor(inner[:, c, :], rth[:, c % 2, :], wkb[:, c % 2, :], ALU.mult), "rwkv")

            def residual(b):
                until(pool, b, "x2_ready")
                raised(pool.tensor_tensor(res[:, :, :], x0[:, :, :], x2[:, :, :], ALU.add), "residual")

            pool.wait_ge(setup["loaded"], ALL_LOADED)
            def expert(b, e):
                if e % 2:
                    until(pool, b, "spread_out", e // 2 + 1)
                    raised(pool.tensor_tensor(ug[:, e % 4, :], xdT[:, :], spread[e // 2 % 2], ALU.mult), "ug_side")

            turns(pool, {
                **each("expert", NE, expert),
                **{f"norm{n}": (lambda b, n=n: inverse_root(b, n)) for n in (1, 2, 3, 4, 6, 7)},
                "norm0": lambda b: (inverse_root(b, 0), first_gain(b)), "norm5": inverse_rms,
                "rope": rope_sum, "parts": parts, **each("read", C, read), "moments2": residual,
            })

        @block.scalar
        def _(act):
            act.wait_ge(setup["loaded"], ALL_LOADED)
            act.wait_ge(setup["ident"], 6)
            act.activation(dec_e[:, :], tdec[:, :], ACT.Exp).then_inc(setup["decay1"], 1)
            act.activation(first[:, :], tfirst[:, :], ACT.Exp).then_inc(setup["decay1"], 1)
            act.wait_ge(setup["decay1"], 2)
            act.activation(decay[:, :], dec_e[:, :], ACT.Exp, scale=-1.0).then_inc(setup["decay"], 1)
            for n, (_, rows, dst) in enumerate(TURNS):
                act.wait_ge(setup["turned_ps"], n + 1)
                act.activation(dst, bank[n % 8][:, 0:rows], ACT.Copy).then_inc(setup["turned"], 1)
            act.wait_ge(setup["fused_ps"], 1)
            act.activation(w_gate[:, 0:NODES], bank[0][:, 0:NODES], ACT.Copy).then_inc(setup["fused"], 1)
            act.wait_ge(setup["fused_ps"], 2)
            act.activation(w_leaf[:, :, :], bank[1][:, 0:2 * P].rearrange("p (k h) -> p k h", k=2), ACT.Copy).then_inc(setup["fused"], 1)
            act.wait_ge(setup["rot"], 1)
            act.wait_ge(setup["fused"], 2)

            def move(b, dst, src, after, signal, n=None, func=ACT.Identity, **kw):
                until(act, b, after, n)
                raised(act.activation(dst, src, func, **kw), signal)

            def norm(b, n, dst, t, signal):
                ln, k = ln_of(n)
                until(act, b, f"{ln}_rstd" if n == RMS else f"{ln}_shift", k + 1)
                for j in range(J):
                    bias = {} if n == RMS else {"bias": shift[:, n, j:j + 1]}
                    last = act.activation(dst[:, j, :], t[:, j, :], ACT.Identity, scale=rstd[:, n, j:j + 1], **bias)
                raised(last, signal)

            def turn_pre(b):
                move(b, xnT[:, 1:T + 1], W[0], "xnT_ps", "xnT", scale=v_["pre_g"], bias=v_["pre_b"])

            def sums(b, c):
                if c >= 2:
                    until(act, b, "rwkv", c - 1)
                move(b, rth[:, c % 2, :], W[0], "r_ps", "r_tanh", c + 1, func=ACT.Tanh, scale=0.5)
                move(b, kk[:, c % 2, :], kk[:, c % 2, :], "k_clamped", "k_exp", c + 1, func=ACT.Exp)
                until(act, b, "k_exp", c + 1)
                raised(act.activation(wkb[:, c % 2, :], kk[:, c % 2, :], ACT.Identity, scale=first[:, c:c + 1], bias=keps[:, 0:1]), "k_first")

            def channel_in(b, c):
                if c == C:
                    move(b, rth2[:, :], W[0], "cmr_ps", "cmr_tanh", func=ACT.Tanh, scale=0.5)
                    return
                if c >= 2:
                    until(act, b, "silu", c - 1)
                move(b, cth[:, c % 2, :], W[1 + c % 2], "cmk_ps", "cmk_tanh", c + 1, func=ACT.Tanh, scale=0.5)

            def gates(b):
                for k in range(2):
                    move(b, gate[:, 2 * k:2 * k + 2, 0:NODES], W[1 + k].rearrange("p (j n) -> p j n", j=2)[:, :, 0:NODES],
                         "gate_ps", "gate_tanh", k + 1, func=ACT.Tanh, scale=0.5)

            def leaves_out(b):
                for k in range(2):
                    move(b, lpT[:, k, :], W[k], "leafT_ps", "leafT", k + 1)

            def leaf_sum(b):
                move(b, ffnT[:, :], W[2], "ffn_ps", "ffnT", bias=v_["wout_b"])

            def rope_values(b):
                move(b, values[:, :, :], tok(W[2]), "v_tok_ps", "v_out")

            def place_values(b):
                move(b, vaug[:, :, :, 0:DH], values[:, :, :].rearrange("p j (h d) -> p j h d", d=DH), "v_out", "vaug")

            def keep(b):
                until(act, b, "xc_ready")
                raised(act.activation(kept[:, :, :], xc[:, :, :], ACT.Identity), "xc_kept")
                until(act, b, "xc_kept")

            def parts(b):
                until(act, b, "rope_out")
                for t in range(2):
                    raised(act.activation(part[t][0][:, :], qk[t], ACT.Identity), "part1")
                for t in range(2):
                    move(b, part[t][1][:, :], rest[t], "rest1", "part2", t + 1)

            def score(b, n):
                g, u = n // 5, n % 5
                if g:
                    until(act, b, "pv_ps", 3 * g - 2 + (0, 0, 1, 1, 2)[u])
                move(b, prob[:, 2 * u:2 * u + 2, :], SD[n % 2][:, :].rearrange("p (u s) -> p u s", u=2),
                     "score_ps", "prob", n + 1, func=ACT.Exp, scale=float(DH) ** -0.5)

            def expert_weights(b):
                until(act, b, "lshift")
                raised(act.activation(lex[:, :, :], lsh[:, :, :], ACT.Exp), "lexp")

            def last_norm(b):
                if isinstance(b, int) and b == B - 1:
                    until(act, b - 1, "stored")
                norm(b, 7, yo, yd, "out_ready")

            def expert(b, e):
                if e % 2:
                    move(b, spread[e // 2 % 2], S[3], "gb_ps", "spread_out", e + 1)

            turns(act, {
                **each("expert", NE, expert),
                "norm0": lambda b: norm(b, 0, hat, x0, "ln0_hat"), "norm1": lambda b: norm(b, 1, hat, x1, "pre_hat"),
                "norm2": lambda b: norm(b, 2, hat, x2, "post_hat"), "norm3": lambda b: norm(b, 3, xb, y0, "xb_ready"),
                "norm4": lambda b: norm(b, 4, xc, yb, "xc_ready"), "norm5": lambda b: norm(b, 5, xch, xc, "xc_hat"),
                "norm6": lambda b: norm(b, 6, xd, yc, "xd_ready"), "norm7": last_norm,
                "turn_pre": turn_pre, **each("sums", C, sums), "read_out": lambda b: move(b, woT[:, :], W[1], "wo_ps", "woT"),
                "turn_post": lambda b: move(b, xn2T[:, 1:T + 1], W[0], "xn2T_ps", "xn2T", scale=v_["post_g"], bias=v_["post_b"]),
                **each("channel_in", C + 1, channel_in), "turn_tree": lambda b: move(b, xbT[:, :], W[0], "xbT_ps", "xbT"),
                "gates": gates, "leaves": leaves_out, "leaf_sum": leaf_sum,
                "turn_in": lambda b: move(b, xcT[:, :], W[0], "xcT_ps", "xcT", scale=v_["norm_scale"]),
                "rope": rope_values, "parts": parts, "place_values": place_values, "keep": keep,
                "maxima": lambda b: move(b, nmax[:, :], S[0][0:NH, :], "maxT_ps", "negmax", scale=-1.0),
                **each("score", 5 * NQ, score), **each("sum_out", NQ, lambda b, g: move(b, pvT[:, :], O, "pv_ps", "pvT", 3 * g + 3)),
                "project": lambda b: move(b, attT[:, :], S[3], "attnT_ps", "attnT"),
                "turn_experts": lambda b: move(b, xdT[:, :], S[3], "xdT_ps", "xdT"),
                "route": expert_weights, "turn_gates": lambda b: move(b, gT[:, :], S[3][0:PARTS * NE, :], "gT_ps", "gT"),
                "experts_out": lambda b: move(b, moT[:, :], O, "moe_ps", "moeT", bias=bshs[:, 0:1]),
            })

        @block.vector
        def _(dve):
            dve.wait_ge(setup["loaded"], ALL_LOADED)
            dve.tensor_scalar(wo[:, :, :], wo[:, :, :], 0.5, None, ALU.mult).then_inc(setup["scaled"], 1)
            dve.tensor_scalar(cwv[:, :, :], cwv[:, :, :], 0.5, None, ALU.mult).then_inc(setup["scaled"], 1)
            dve.tensor_tensor(wshs, wsh[:, 0, :], wsh[:, 1, :], ALU.add).then_inc(setup["scaled"], 1)
            dve.tensor_tensor(bshs[:, :], bsh[:, 0:1], bsh[:, 1:2], ALU.add).then_inc(setup["scaled"], 1)
            dve.wait_ge(setup["scaled"], 4)
            dve.tensor_scalar(wshs, wshs, 0.5, None, ALU.mult).then_inc(setup["scaled"], 1)
            dve.tensor_scalar(bshs[:, :], bshs[:, :], 0.5, None, ALU.mult).then_inc(setup["scaled"], 1)
            half = DH // 2
            for t, w in enumerate((aq, ak)):
                by_dim = w[:, :].rearrange("p (h d) -> p d h", d=DH)
                dve.tensor_copy(w_rope[:, 2 * t, :, :], by_dim)
                dve.tensor_scalar(w_rope[:, 2 * t + 1, 0:half, :], by_dim[:, half:DH, :], -1.0, None, ALU.mult)
                last = dve.tensor_copy(w_rope[:, 2 * t + 1, half:DH, :], by_dim[:, 0:half, :])
            last.then_inc(setup["rot"], 1)
            def after_steps(n):
                dve.wait_ge(setup["brow_parts"], n)
            dve.tensor_copy(brow_part[:, 0, :], brow).then_inc(setup["brow_parts"], 1)
            after_steps(1)
            dve.tensor_tensor(brow_rest, brow, brow_part[:, 0, :], ALU.subtract).then_inc(setup["brow_parts"], 1)
            after_steps(2)
            dve.tensor_copy(brow_part[:, 1, :], brow_rest).then_inc(setup["brow_parts"], 1)
            after_steps(3)
            dve.tensor_tensor(brow_part[:, 2, :], brow_rest, brow_part[:, 1, :], ALU.subtract).then_inc(setup["brow_parts"], 1)
            after_steps(4)
            dve.wait_ge(setup["ident"], 6)
            dve.tensor_tensor(brow_rest[:, 0:NE], ident[0:PARTS * NE, 0:NE], ident[0:PARTS * NE, NE:2 * NE], ALU.add).then_inc(setup["brow_parts"], 1)
            after_steps(5)
            dve.tensor_tensor(owner[:, :], brow_rest[:, 0:NE], ident[0:PARTS * NE, 2 * NE:3 * NE], ALU.add).then_inc(setup["brow_parts"], 1)
            dve.wait_ge(setup["decay"], 1)
            dve.wait_ge(setup["rot"], 1)
            dve.wait_ge(setup["ident"], 6)

            def moments(b, n, t):
                ln, k = ln_of(n)
                for j in range(J):
                    last = dve.bn_stats(stats[:, n, j, :], t[:, j, :])
                raised(last, f"{ln}_stats")
                until(dve, b, f"{ln}_stats", k + 1)
                apart(dve)
                for j in range(J):
                    last = dve.bn_aggr(mv[:, n, j, :], stats[:, n, j, :])
                raised(last, f"{ln}_moments")

            def stt(out_, in0, scalar, in1, op0, op1):
                return dve.scalar_tensor_tensor(out=out_, in0=in0, scalar=scalar, in1=in1, op0=op0, op1=op1)

            def mix(b, xT, diff, dst, ready, differ, signal, amounts):
                until(dve, b, ready)
                raised(dve.tensor_tensor(diff[:, :], xT[:, 1:T + 1], xT[:, 0:T], ALU.subtract), differ)
                until(dve, b, differ)
                for t, m in zip(dst, amounts):
                    raised(stt(t[:, :], diff[:, :], v_[m], xT[:, 0:T], ALU.mult, ALU.add), signal)

            def clamp(b, c):
                until(dve, b, "k_ps", c + 1)
                if c >= 2:
                    until(dve, b, "k_first", c - 1)
                raised(dve.tensor_scalar(kk[:, c % 2, :], W[1], K_CLAMP, None, ALU.min), "k_clamped")

            def sums(b, c):
                until(dve, b, "v_ps", c + 1)
                until(dve, b, "k_exp", c + 1)
                raised(dve.tensor_tensor(kvb[:, c % 2, :], kk[:, c % 2, :], W[2], ALU.mult), "kv")
                dc = decay[:, c:c + 1].broadcast_to([P, T])
                raised(dve.tensor_tensor_scan(ksum[:, c % 2, 1:T + 1], dc, kk[:, c % 2, :], 0.0, ALU.mult, ALU.add), "k_sum")
                until(dve, b, "kv", c + 1)
                raised(dve.tensor_tensor_scan(kvsum[:, c % 2, 1:T + 1], dc, kvb[:, c % 2, :], 0.0, ALU.mult, ALU.add), "kv_sum")

            def read(b, c):
                until(dve, b, "kv_sum", c + 1)
                raised(stt(kvb[:, c % 2, :], kvb[:, c % 2, :], first[:, c:c + 1], kvsum[:, c % 2, 0:T], ALU.mult, ALU.add), "wkv")
                until(dve, b, "wk", c + 1)
                raised(dve.reciprocal(wkb[:, c % 2, :], wkb[:, c % 2, :]), "wk_inv")

            def first_moments(b):
                dve.wait_ge(sems["x_loaded"], b * 16 + 16)
                moments(b, 0, x0)

            def second_moments(b):
                until(dve, b, "x1_ready")
                moments(b, 1, x1)

            def post_moments(b):
                until(dve, b, "wo_tok_ps")
                raised(dve.tensor_tensor(x2[:, :, :], x1[:, :, :], tok(W[2]), ALU.add), "x2_ready")
                until(dve, b, "x2_ready")
                moments(b, 2, x2)

            def channel_in(b, c):
                until(dve, b, "cmk_tanh", c + 1)
                raised(stt(inner[:, c, :], cth[:, c % 2, :], 1.0, W[1 + c % 2], ALU.add, ALU.mult), "silu")

            def channel_out(b):
                until(dve, b, "cmr_tanh")
                until(dve, b, "cmv_ps")
                raised(stt(cmT[:, :], rth2[:, :], 0.5, W[1], ALU.mult, ALU.add), "cmixT")

            def tree_moments(b):
                until(dve, b, "cmix_tok_ps")
                until(dve, b, "residual")
                raised(stt(y0[:, :, :], tok(W[2]), 0.5, res[:, :, :], ALU.add, ALU.add), "y0")
                until(dve, b, "y0")
                moments(b, 3, y0)

            def tree_gates(b):
                until(dve, b, "gate_tanh")
                raised(dve.tensor_scalar(gate[:, :, 0:NODES], gate[:, :, 0:NODES], 0.5, 0.5, ALU.mult, ALU.add), "gate")

            def tree(b, level):
                src, dst = ((lpa, lpb), (lpb, lpa))[level % 2]
                n = 2 ** level
                g = gate[:, :, n - 1:2 * n - 1]
                pair = dst[:, :, 0:2 * n].rearrange("p j (n s) -> p j n s", s=2)
                if level == 0:
                    until(dve, b, "gate")
                    dve.tensor_copy(pair[:, :, :, 1], g)
                    raised(dve.tensor_scalar(pair[:, :, :, 0], g, -1.0, 1.0, ALU.mult, ALU.add), "leaf")
                else:
                    until(dve, b, "leaf", 2 * level - 1)
                    raised(dve.tensor_tensor(pair[:, :, :, 1], src[:, :, 0:n], g, ALU.mult), "leaf")
                    until(dve, b, "leaf", 2 * level)
                    raised(dve.tensor_tensor(pair[:, :, :, 0], src[:, :, 0:n], pair[:, :, :, 1], ALU.subtract), "leaf")

            def after_tree(b):
                until(dve, b, "ffn_tok_ps")
                raised(dve.tensor_tensor(yb[:, :, :], xb[:, :, :], tok(W[0]), ALU.add), "yb")
                until(dve, b, "yb")
                moments(b, 4, yb)

            def rope_products(b):
                for i in range(4):
                    until(dve, b, "rope_ps", i + 1)
                    raised(dve.tensor_tensor(rope[i][:, :], (cos_t if i % 2 == 0 else sin_t)[:, :], W[ROPE_BANK[i]], ALU.mult), "rope_mul")

            def row_maxima(b, h):
                for n, j in enumerate(TILE_ORDER):
                    until(dve, b, "rowscore_ps", h * J + (1, 3, 3, 4)[n])
                    raised(dve.tensor_reduce(rmax[:, j, h:h + 1], row_place(j), AX_X, ALU.max), "rowmax")

            def maxima(b):
                until(dve, b, "negmax")
                raised(dve.tensor_copy(mpart[0][:, :], nmax[:, :]), "max_parts")
                until(dve, b, "max_parts", 1)
                raised(dve.tensor_tensor(mrest, nmax[:, :], mpart[0][:, :], ALU.subtract), "max_rest")
                until(dve, b, "max_rest", 1)
                raised(dve.tensor_copy(mpart[1][:, :], mrest), "max_parts")
                until(dve, b, "max_parts", 2)
                raised(dve.tensor_tensor(mpart[2][:, :], mrest, mpart[1][:, :], ALU.subtract), "max_parts")

            def attended(b, g):
                until(dve, b, "pv_tok_ps", g + 1)
                o = tok(O).rearrange("p j (g r) -> p j g r", r=32)
                raised(dve.reciprocal(pvi[:, :, :], o[:, :, :, DH]), "pv_inv")
                until(dve, b, "pv_inv", g + 1)
                raised(dve.tensor_tensor(att[:, :, :].rearrange("p j (h d) -> p j h d", d=DH)[:, :, 4 * g:4 * g + 4, :], o[:, :, :, 0:DH],
                                         pvi[:, :, :].rearrange("p j (g o) -> p j g o", o=1).broadcast_to([P, J, 4, DH]), ALU.mult), "attn")

            def expert_moments(b):
                until(dve, b, "proj_ps")
                raised(dve.tensor_tensor(yc[:, :, :], kept[:, :, :], tok(S[3]), ALU.add), "yc")
                until(dve, b, "yc")
                moments(b, 6, yc)

            def route_softmax(b):
                until(dve, b, "logit_ps")
                ps_lg = S[3][:, 0:J * NE].rearrange("p (j e) -> p j e", j=J)
                raised(dve.tensor_tensor(lg[:, :, :], ps_lg, ebias[:, :].rearrange("p (o e) -> p o e", o=1).broadcast_to([P, J, NE]), ALU.add), "logits")
                until(dve, b, "logits")
                raised(dve.tensor_reduce(lm[:, :], lg[:, :, :], AX_X, ALU.max), "lmax")
                until(dve, b, "lmax")
                raised(dve.tensor_tensor(lsh[:, :, :], lg[:, :, :], wide(lm[:, :], NE), ALU.subtract), "lshift")

            def route_probs(b):
                until(dve, b, "lexp")
                raised(dve.tensor_reduce(lsu[:, :], lex[:, :, :], AX_X, ALU.add), "lsum")
                until(dve, b, "lsum")
                raised(dve.reciprocal(lin[:, :], lsu[:, :]), "linv")
                until(dve, b, "linv")
                raised(dve.tensor_tensor(pe_[:, :, :], lex[:, :, :], wide(lin[:, :], NE), ALU.mult), "prob_e")

            ranks = rank[:, :].rearrange("p (o e) -> p o e", o=1).broadcast_to([P, J, NE])

            def largest(b, n):
                step, second = n % 5, n // 5
                s, m, eq, key, km, hot = ((pe_, m1, eq1, key1, km1, hot1), (left, m2, eq2, key2, km2, hot2))[second]
                done = 5 * second
                if step == 0:
                    until(dve, b, "pick", 5) if second else until(dve, b, "prob_e")
                    ins = dve.tensor_reduce(m[:, :], s[:, :, :], AX_X, ALU.max)
                elif step == 4:
                    until(dve, b, "pick", done + 4)
                    raised(dve.tensor_tensor(hot[:, :, :], key[:, :, :], wide(km[:, :], NE), ALU.is_equal), "hot")
                    return
                else:
                    until(dve, b, "pick", done + step)
                    ins = (lambda: dve.tensor_tensor(eq[:, :, :], s[:, :, :], wide(m[:, :], NE), ALU.is_equal),
                           lambda: dve.tensor_tensor(key[:, :, :], eq[:, :, :], ranks, ALU.mult),
                           lambda: dve.tensor_reduce(km[:, :], key[:, :, :], AX_X, ALU.max))[step - 1]()
                raised(ins, "pick")

            def others(b):
                until(dve, b, "hot", 1)
                raised(stt(left[:, :, :], hot1[:, :, :], -2.0, pe_[:, :, :], ALU.mult, ALU.add), "pick")

            def gates_of_both(b):
                until(dve, b, "hot", 2)
                raised(dve.tensor_tensor(hots[:, :, :], hot1[:, :, :], hot2[:, :, :], ALU.add), "hot")
                until(dve, b, "hot", 3)
                raised(dve.tensor_tensor(gts[:, :, :], pe_[:, :, :], hots[:, :, :], ALU.mult), "gates")

            def gate_parts(b):
                until(dve, b, "gates")
                raised(dve.tensor_copy(gate_part[:, :, 0, :], gts[:, :, :]), "gate_part")
                until(dve, b, "gate_part", 1)
                raised(dve.tensor_tensor(gate_rest[:, :, :], gts[:, :, :], gate_part[:, :, 0, :], ALU.subtract), "gate_part")
                until(dve, b, "gate_part", 2)
                raised(dve.tensor_copy(gate_part[:, :, 1, :], gate_rest[:, :, :]), "gate_part")
                until(dve, b, "gate_part", 3)
                raised(dve.tensor_tensor(gate_part[:, :, 2, :], gate_rest[:, :, :], gate_part[:, :, 1, :], ALU.subtract), "gate_part")

            def expert(b, e):
                if e % 2:
                    return
                until(dve, b, "gb_ps", e + 1)
                raised(dve.tensor_tensor(ug[:, e % 4, :], xdT[:, :], S[3], ALU.mult), "ug")

            def last_moments(b):
                until(dve, b, "moe_tok_ps")
                raised(stt(yd[:, :, :], xd[:, :, :], 2.0, tok(O), ALU.mult, ALU.add), "yd")
                until(dve, b, "yd")
                moments(b, 7, yd)

            turns(dve, {
                "mix": lambda b: mix(b, xnT, dif, mixed, "xnT", "mix_diff", "mixed", ("mix_k", "mix_v", "mix_r")),
                "mix2": lambda b: mix(b, xn2T, dif2, mixed2, "xn2T", "mix2_diff", "mixed2", ("cmix_k", "cmix_r")),
                "moments0": first_moments,
                "moments1": second_moments,

                **each("clamp", C, clamp), **each("sums", C, sums), **each("read", C, read),
                "moments2": post_moments,

                **each("channel_in", C, channel_in), "channel_out": channel_out,
                "moments3": tree_moments,
                "tree": tree_gates, **each("level", 8, tree), "moments4": after_tree,
                "moments5": lambda b: (until(dve, b, "xc_ready"), moments(b, 5, xc)),
                "rope": rope_products, **each("rowmax", NH, row_maxima), "maxima": maxima, **each("back", NQ, attended),
                "moments6": expert_moments,
                "route": route_softmax, "route_probs": route_probs, **each("largest", 10, largest),
                "others": others, "route_gates": gates_of_both, "gate_parts": gate_parts, **each("expert", NE, expert),
                "moments7": last_moments,
            })

        @block.tensor
        def _(pe):
            pe.wait_ge(setup["ident"], 6)
            pe.wait_ge(setup["loaded"], ALL_LOADED)
            pe.wait_ge(setup["scaled"], 6)
            pe.wait_ge(setup["rot"], 1)
            pe.wait_ge(setup["brow_parts"], 6)
            for n, (src, rows, _) in enumerate(TURNS):
                if n >= 8:
                    pe.wait_ge(setup["turned"], n - 7)
                pe.transpose(bank[n % 8][:, 0:rows], src, ident[0:rows, 0:rows]).then_inc(setup["turned_ps"], 1)
            pe.wait_ge(setup["turned"], len(TURNS))
            pe.matmul(bank[0][:, 0:NODES], tq, routersT[:, 0:NODES], start=True, stop=True).then_inc(setup["fused_ps"], 1)
            for k in range(2):
                last = pe.matmul(bank[1][:, k * P:(k + 1) * P], leavesT[:, k * P:(k + 1) * P], woutT, start=True, stop=True)
            last.then_inc(setup["fused_ps"], 1)
            pe.wait_ge(setup["fused"], 2)

            def turn(bk, t, signal):
                for j in range(J):
                    last = pe.transpose(bk[:, j * P:(j + 1) * P], t[:, j, :], ident[:, :])
                raised(last, signal)

            def mm(out_, w, x, start=True, stop=True, **kw):
                return pe.matmul(out_, w, x, start=start, stop=stop, **kw)

            def tiles(t):
                return t[:, :].rearrange("p (j h) -> p j h", j=J)

            def turn_when(ready, bk, t, signal):
                return lambda b: (until(pe, b, ready), turn(bk, t, signal))

            def project(b, c):
                cs = slice(c * P, (c + 1) * P)
                for i, (w, bk, done, freed) in enumerate(((wk, W[1], "k_ps", "k_clamped"), (wv, W[2], "v_ps", "kv"), (wr, W[0], "r_ps", "r_tanh"))):
                    until(pe, b, "mixed", i + 1) if c == 0 else until(pe, b, freed, c)
                    raised(mm(bk, w[:, cs], mixed[i][:, :]), done)

            def read_out(b):
                until(pe, b, "k_clamped")
                for c in range(C):
                    until(pe, b, "rwkv", c + 1)
                    last = mm(W[1], wo[:, c, :], inner[:, c, :], c == 0, c == C - 1)
                raised(last, "wo_ps")

            def channel_in(b, c):
                if c == C:
                    until(pe, b, "mixed2", 2)
                    raised(mm(W[0], cwr[:, :], mixed2[1][:, :]), "cmr_ps")
                    return
                until(pe, b, "silu", c - 1) if c >= 2 else until(pe, b, "mixed2", 1)
                raised(mm(W[1 + c % 2], cwk[:, c * P:(c + 1) * P], mixed2[0][:, :]), "cmk_ps")

            def channel_out(b):
                for c in range(C):
                    until(pe, b, "silu", max(c + 1, 3))
                    last = mm(W[1], cwv[:, c, :], inner[:, c, :], c == 0, c == C - 1)
                raised(last, "cmv_ps")

            def gates(b):
                until(pe, b, "xbT")
                for k in range(2):
                    for j in range(2 * k, 2 * k + 2):
                        last = mm(W[1 + k][:, (j % 2) * LEAVES:(j % 2) * LEAVES + NODES], xbT[:, j * P:(j + 1) * P], w_gate[:, 0:NODES])
                    raised(last, "gate_ps")

            def leaves_out(b):
                until(pe, b, "leaf")
                for k in range(2):
                    turn(W[k], lpa[:, :, k * P:(k + 1) * P], "leafT_ps")

            def leaf_sum(b):
                for k in range(2):
                    until(pe, b, "leafT", k + 1)
                    last = mm(W[2], w_leaf[:, k, :], lpT[:, k, :], k == 0, k == 1)
                raised(last, "ffn_ps")

            def rope_products(b):
                until(pe, b, "xcT")
                for i in range(4):
                    if i == 3:
                        until(pe, b, "rope_mul", 1)
                    raised(mm(W[ROPE_BANK[i]], w_rope[:, i, :, :].rearrange("p d h -> p (d h)"), xcT[:, :]), "rope_ps")
                until(pe, b, "rope_mul", 2)
                for j in range(J):
                    last = mm(W[2][:, j * P:(j + 1) * P], xcT[:, j * P:(j + 1) * P], av[:, :])
                raised(last, "v_tok_ps")

            def row_scores(b, h):
                if h == 0:
                    until(pe, b, "rope_mul")
                    until(pe, b, "heads_in")
                for n, j in enumerate(TILE_ORDER):
                    if h and n != 1:
                        until(pe, b, "rowmax", (h - 1) * J + {0: 1, 2: 3, 3: 4}[n])
                    elif h:
                        until(pe, b, "rowmax", (h - 1) * J + 3)
                    q, to = qh[0:KROWS, h, j * P:(j + 1) * P], row_place(j)
                    mm(to, q, kh[0:KROWS, h, 0:(j + 1) * P], True, False, skip_group_check=True)
                    raised(mm(to[:, j * P:(j + 1) * P], identb[:, :], maskb[:, :], False, True, skip_group_check=True), "rowscore_ps")

            def maxima(b):
                until(pe, b, "rowmax")
                for j in range(J):
                    last = pe.transpose(S[0][0:NH, j * P:(j + 1) * P], rmax[:, j, :], ident[:, :])
                raised(last, "maxT_ps")

            def score(b, n):
                g, u = n // 5, n % 5
                if n == 0:
                    until(pe, b, "negmax")
                    until(pe, b, "max_in")
                elif n >= 2:
                    until(pe, b, "prob", n - 1)
                for s in range(2):
                    bk = SD[n % 2][:, s * T:(s + 1) * T]
                    h = 4 * g + 2 * (u % 2) + s
                    for head, i, col in ([(h, 0, 0)], [(h, 1, 0), (h, 3, 3 * P)], [(4 * g + 2 * s, 2, 0), (4 * g + 2 * s + 1, 2, 2 * P)])[u // 2]:
                        mm(bk[:, col:col + T - i * P], kh[:, head, i * P:(i + 1) * P], qh[:, head, i * P:T], True, False, skip_group_check=True)
                        last = mm(bk[:, col:col + P], identb[:, :], maskTb[:, :], False, True, skip_group_check=True)
                raised(last, "score_ps")

            def weigh(b, g):
                until(pe, b, "vaug") if g == 0 else until(pe, b, "attn", g)
                for i, pairs, unit in ((0, 2, lambda q: (q, 0)), (1, 4, lambda q: (4 + q, 0)), (3, 4, lambda q: (4 + q, 3 * P)),
                                       (2, 5, lambda q: (8 + q // 2, (q % 2) * 2 * P))):
                    if i != 3:
                        until(pe, b, "prob", 5 * g + pairs)
                    for q in range(4):
                        u, col = unit(q)
                        last = mm(O[32 * q:32 * q + 32, i * P:T], vaug[:, i, 4 * g + q, :], prob[:, u, col:col + T - i * P],
                                  i == 0, i == 2, tile_position=(0, 32 * q), skip_group_check=True)
                    if i != 1:
                        raised(last, "pv_ps")

            def attn_project(b):
                until(pe, b, "attn")
                until(pe, b, "prob")
                turn(S[3], att, "attnT_ps")

            def attn_out(b):
                until(pe, b, "attnT")
                for j in range(J):
                    last = mm(S[3][:, j * P:(j + 1) * P], attT[:, j * P:(j + 1) * P], ao[:, :])
                raised(last, "proj_ps")

            def turn_experts(b):
                until(pe, b, "xd_ready")
                turn(S[3], xd, "xdT_ps")

            def centroids(b):
                until(pe, b, "xdT")
                for j in range(J):
                    last = mm(S[3][:, j * NE:(j + 1) * NE], xdT[:, j * P:(j + 1) * P], centT[:, :])
                raised(last, "logit_ps")

            def turn_gates(b):
                until(pe, b, "gate_part")
                for j in range(J):
                    last = mm(S[3][0:PARTS * NE, j * P:(j + 1) * P], gate_part[:, j, :, :].rearrange("p i e -> p (i e)"), identb[:, :])
                raised(last, "gT_ps")

            def start_experts(b):
                mm(O, wshT[:, :], xdT[:, :], True, False, skip_group_check=True)
                until(pe, b, "gT")
                for i in range(PARTS):
                    mm(O, brow_part[:, i, :], gT[:, :], False, False, skip_group_check=True)

            def product(b, e):
                until(pe, b, ("ug", "ug_side")[e % 2], e // 2 + 1)
                return mm(O, wexpT[:, e, :], ug[:, e % 4, :], False, e == NE - 1, skip_group_check=True)

            def expert(b, e):
                if e:
                    until(pe, b, ("ug", "spread_out")[(e - 1) % 2], (e - 1) // 2 + 1)
                raised(mm(S[3], owner[:, e:e + 1].broadcast_to([PARTS * NE, P]), gT[:, :]), "gb_ps")
                if e >= 2:
                    product(b, e - 2)

            def experts_out(b):
                product(b, NE - 2)
                raised(product(b, NE - 1), "moe_ps")

            turns(pe, {
                "turn_pre": turn_when("pre_hat", W[0], hat, "xnT_ps"), **each("project", C, project), "read_out": read_out,
                "read_turn": turn_when("woT", W[2], tiles(woT), "wo_tok_ps"),
                "turn_post": turn_when("post_hat", W[0], hat, "xn2T_ps"), **each("channel_in", C + 1, channel_in),
                "channel_out": channel_out, "channel_turn": turn_when("cmixT", W[2], tiles(cmT), "cmix_tok_ps"),
                "turn_tree": turn_when("xb_ready", W[0], xb, "xbT_ps"), "gates": gates, "leaves": leaves_out, "leaf_sum": leaf_sum, "leaf_turn": turn_when("ffnT", W[0], tiles(ffnT), "ffn_tok_ps"),
                "turn_in": turn_when("xc_hat", W[0], xch, "xcT_ps"), "rope": rope_products, **each("rowmax", NH, row_scores),
                "maxima": maxima, **each("score", 5 * NQ, score), **each("weigh", NQ, weigh),
                **each("back", NQ, lambda b, g: (until(pe, b, "pvT", g + 1), turn(O, tiles(pvT), "pv_tok_ps"))),
                "project": attn_project, "attn_out": attn_out, "turn_experts": turn_experts, "centroids": centroids, "turn_gates": turn_gates,
                "start_experts": start_experts, **each("expert", NE, expert), "experts_out": experts_out,
                "experts_turn": turn_when("moeT", O, tiles(moT), "moe_tok_ps"),
                "o_free": lambda b: until(pe, b, "yd"),
                "w_free": lambda b: (until(pe, b, "rope_mul"), until(pe, b, "v_out")),
            })


_UNUSED = ["L0_ffn_leaf_keys"]
_ROPE_BASE = 1000000.0


def _rope_tables():
    import numpy as np
    half = DH // 2
    theta = (1.0 / np.power(np.float32(_ROPE_BASE), (2 * np.arange(half) / DH).astype(np.float32))).astype(np.float32)
    angles = (theta[:, None] * np.arange(T, dtype=np.float32)[None, :]).astype(np.float32)
    rows = np.repeat(np.tile(angles, (2, 1)), NH, axis=0)
    return np.cos(rows).astype(np.float32), np.sin(rows).astype(np.float32)


def kernel(**inputs):
    import numpy as _np
    import concourse.bacc as _bacc
    from concourse.bass_utils import run_bass_kernel_spmd as _run

    nc = _bacc.Bacc("TRN2", target_bir_lowering=False, num_devices=1)
    arrays, args = {}, {}
    given = {n: _np.ascontiguousarray(v) for n, v in inputs.items() if n not in _UNUSED}
    given["rope_cos"], given["rope_sin"] = _rope_tables()
    for name, v in given.items():
        arrays[f"in_{name}_dram"] = v
        args[name] = nc.dram_tensor(f"in_{name}_dram", v.shape, mybir.dt.from_np(v.dtype), kind="ExternalInput").ap()
    out = nc.dram_tensor("out_0_dram", (B, T, P), F32, kind="ExternalOutput").ap()
    build(nc, args, out)
    r = _run(nc, [arrays], core_ids=[0])
    return r.results[0]["out_0_dram"]
```
